# Optimizing a Trainium2 kernel written in Bass

```python
import numpy as np
import jax
import jax.numpy as jnp

def _softmax(x, axis=-1):
    return jax.nn.softmax(x, axis=axis)

def _gelu(x):
    return jax.nn.gelu(x, approximate=True)

def _silu(x):
    return jax.nn.silu(x)

def _sigmoid(x):
    return jax.nn.sigmoid(x)

def _layernorm(x, axis=-1, eps=1e-05):
    m = jnp.mean(x, axis=axis, keepdims=True)
    v = jnp.var(x, axis=axis, keepdims=True)
    return (x - m) / jnp.sqrt(v + eps)

def _scatter_add(tgt, idx, src, axis=0):
    return tgt.at[idx].add(src)

def _segment_sum(src, seg, n):
    return jax.ops.segment_sum(src, seg, n)
kernel_name = 'mk_gnn_resnorm_d1_gnn_r32_5a24e3'

def setup_inputs(seed: int=0):
    np.random.seed(seed)
    _w = jnp.asarray

    def _rec_inputs():
        import jax
        import jax.numpy as jnp
        _gk = jax.random.key(seed)
        x = -0.0003713 + 1 * jax.random.normal(jax.random.fold_in(_gk, 1), (50000, 256), jnp.float32)
        src = jax.random.randint(jax.random.fold_in(_gk, 2), (25000,), 0, 50000, jnp.int32)
        dst = jax.random.randint(jax.random.fold_in(_gk, 3), (25000,), 0, 50000, jnp.int32)
        _o = jnp.argsort(dst, stable=True)
        src = src[_o]
        dst = dst[_o]
        return (x, src, dst)
    x, src, dst = _rec_inputs()

    def _L0_gnn_setup():
        import jax, jax.numpy as jnp
        import numpy as np
        N = 50000
        E = 15625
        D = 256
        key = jax.random.key(seed)
        ks = jax.random.split(key, 12)
        s = 0.02
        x = jax.random.normal(ks[0], (N, D), dtype=jnp.float32)
        edge_index = jax.random.randint(ks[1], (2, E), 0, N, dtype=jnp.int64)
        W1 = jax.random.normal(ks[2], (D, 2 * D), dtype=jnp.float32) * s
        b1 = jax.random.normal(ks[3], (D,), dtype=jnp.float32) * s
        W2 = jax.random.normal(ks[4], (D, D), dtype=jnp.float32) * s
        b2 = jax.random.normal(ks[5], (D,), dtype=jnp.float32) * s
        w_ih = jax.random.normal(ks[6], (3 * D, D), dtype=jnp.float32) * s
        w_hh = jax.random.normal(ks[7], (3 * D, D), dtype=jnp.float32) * s
        b_ih = jax.random.normal(ks[8], (3 * D,), dtype=jnp.float32) * s
        b_hh = jax.random.normal(ks[9], (3 * D,), dtype=jnp.float32) * s
        gamma = jnp.ones((D,), dtype=jnp.float32)
        beta = jnp.zeros((D,), dtype=jnp.float32)
        return {'x': x, 'edge_index': edge_index, 'W1': W1, 'b1': b1, 'W2': W2, 'b2': b2, 'w_ih': w_ih, 'w_hh': w_hh, 'b_ih': b_ih, 'b_hh': b_hh, 'gamma': gamma, 'beta': beta}
    _L0_gnn_all = _L0_gnn_setup()
    _L0_gnn_in = {k: v for k, v in _L0_gnn_all.items() if k in ('W1', 'b1', 'W2', 'b2', 'w_ih', 'w_hh', 'b_ih', 'b_hh', 'gamma', 'beta')}
    del _L0_gnn_all
    return {'x': x, 'src': src, 'dst': dst, 'L0_gnn_W1': _L0_gnn_in['W1'], 'L0_gnn_b1': _L0_gnn_in['b1'], 'L0_gnn_W2': _L0_gnn_in['W2'], 'L0_gnn_b2': _L0_gnn_in['b2'], 'L0_gnn_w_ih': _L0_gnn_in['w_ih'], 'L0_gnn_w_hh': _L0_gnn_in['w_hh'], 'L0_gnn_b_ih': _L0_gnn_in['b_ih'], 'L0_gnn_b_hh': _L0_gnn_in['b_hh'], 'L0_gnn_gamma': _L0_gnn_in['gamma'], 'L0_gnn_beta': _L0_gnn_in['beta']}

def reference(x, src, dst, L0_gnn_W1, L0_gnn_b1, L0_gnn_W2, L0_gnn_b2, L0_gnn_w_ih, L0_gnn_w_hh, L0_gnn_b_ih, L0_gnn_b_hh, L0_gnn_gamma, L0_gnn_beta):
    import jax
    import jax.numpy as jnp

    def _L0_gnn_ref(x, edge_index, W1, b1, W2, b2, w_ih, w_hh, b_ih, b_hh, gamma, beta):
        import jax, jax.numpy as jnp
        import numpy as np
        N = 50000
        E = 15625
        D = 256
        n_nodes = x.shape[0]
        row, col = (edge_index[0], edge_index[1])
        h = jnp.concatenate([x[row], x[col]], axis=-1)
        msgs = jax.nn.silu(h @ W1.T + b1) @ W2.T + b2
        agg = jax.ops.segment_sum(msgs, row, num_segments=n_nodes)
        cnt = jax.ops.segment_sum(jnp.ones((row.shape[0], 1), x.dtype), row, num_segments=n_nodes)
        agg = agg / (cnt + 1e-08)
        gi = agg @ w_ih.T + b_ih
        gh = x @ w_hh.T + b_hh
        i_r, i_z, i_n = jnp.split(gi, 3, axis=-1)
        h_r, h_z, h_n = jnp.split(gh, 3, axis=-1)
        r = jax.nn.sigmoid(i_r + h_r)
        z = jax.nn.sigmoid(i_z + h_z)
        n = jnp.tanh(i_n + r * h_n)
        x_new = (1.0 - z) * n + z * x
        mu = jnp.mean(x_new, axis=-1, keepdims=True)
        var = jnp.var(x_new, axis=-1, keepdims=True)
        return gamma * (x_new - mu) / jnp.sqrt(var + 1e-05) + beta
    edge_index = jnp.stack([src, dst])
    x = _layernorm(x + _L0_gnn_ref(x, edge_index, L0_gnn_W1, L0_gnn_b1, L0_gnn_W2, L0_gnn_b2, L0_gnn_w_ih, L0_gnn_w_hh, L0_gnn_b_ih, L0_gnn_b_hh, L0_gnn_gamma, L0_gnn_beta), axis=-1)
    return x

_drawn_inputs = setup_inputs


def setup_inputs(seed=0):
    import zlib

    import numpy as np

    out = dict(_drawn_inputs(seed))
    spreads = {'L0_gnn_gamma': (1.0, 0.2), 'L0_gnn_beta': (0.0, 0.1)}
    factors = {'L0_gnn_W1': 7.124,
     'L0_gnn_b1': 8.0,
     'L0_gnn_W2': 6.93,
     'L0_gnn_b2': 8.0,
     'L0_gnn_w_ih': 6.699,
     'L0_gnn_b_ih': 5.35,
     'L0_gnn_b_hh': 8.0}
    for name, (base, spread) in spreads.items():
        noise = np.random.default_rng([zlib.crc32(name.encode()), seed]).standard_normal(out[name].shape)
        drawn = base * np.exp(spread * noise) if base else spread * noise
        out[name] = jnp.asarray(drawn.astype(out[name].dtype))
    for name, factor in factors.items():
        out[name] = (out[name] * factor).astype(out[name].dtype)
    return out
```

```python
from contextlib import ExitStack

import concourse.bass as bass
from concourse import mybir

F32 = mybir.dt.float32
F32R = mybir.dt.float32r
BF16 = mybir.dt.bfloat16
I32 = mybir.dt.int32
ALU = mybir.AluOpType
ACT = mybir.ActivationFunctionType

P = 128
D = 256
KD = D // P
GATES = 3 * KD
EPS_COUNT = 1e-8
EPS_NORM = 1e-5

TILES = 2
PAIR = TILES * P
BLOCK = 512
ROWS = BLOCK // P

HH, IH, W1C = 0, KD * GATES * P, 2 * KD * GATES * P
W_COLS = W1C + 2 * KD * KD * P
BANK = 512


class Gate:

    def __init__(self, engine, passed):
        self.engine, self.passed = engine, passed

    def take_waits(self):
        self.engine.sem_inc(self.passed, 1)


class Turn:

    def __init__(self, i, c):
        self.i, self.c = i, c

    def at(self, d):
        return Turn(self.i, self.c + d)

    @property
    def n(self):
        return 2 * self.i + self.c

    @property
    def slot(self):
        return self.c % 2

    @property
    def use(self):
        return self.i + self.c // 2


def gnn_layer(nc, x, src, dst, w1, b1, w2, b2, w_ih, w_hh, b_ih, b_hh, gamma, beta, out):
    N, E = x.shape[0], src.shape[0]
    per_partition = -(-E // P)
    per_partition += per_partition % TILES
    pairs = per_partition // TILES
    full = E // per_partition
    rest = E - full * per_partition
    blocks = -(-N // BLOCK)
    last_parts = (N - (blocks - 1) * BLOCK) // ROWS
    spare = N
    agg_rows = N + P
    count_cols = blocks * ROWS
    assert (N + P) <= blocks * BLOCK + P and spare + P - 1 < blocks * BLOCK

    agg = nc.dram_tensor("agg", (agg_rows, D), F32).ap()

    with ExitStack() as whole:
        def keep(name, shape, dt):
            return whole.enter_context(nc.sbuf_tensor(name, shape, dt))

        ident = keep("ident", [P, P], F32)
        w_hi = keep("w_hi", [P, W_COLS], F32R)
        w_lo = keep("w_lo", [P, W_COLS], F32R)
        gate_bias = keep("gate_bias", [P, 2, GATES], F32)
        rz_bias = keep("rz_bias", [P, 2 * KD], F32)
        inv_count = keep("inv_count", [P, count_cols], F32)
        gamma_b = keep("gamma_b", [P, D], F32)
        beta_b = keep("beta_b", [P, D], F32)
        ps_a = whole.enter_context(nc.psum_tensor("ps_a", [P, 2, BANK], F32))
        ps_b = whole.enter_context(nc.psum_tensor("ps_b", [P, 2, BANK], F32))
        ps_c = whole.enter_context(nc.psum_tensor("ps_c", [P, BANK], F32))
        ps_d = whole.enter_context(nc.psum_tensor("ps_d", [P, BANK], F32))
        ps_e = whole.enter_context(nc.psum_tensor("ps_e", [P, BANK], F32))
        ps_f = whole.enter_context(nc.psum_tensor("ps_f", [P, BANK], F32))

        edge_part(nc, x, src, dst, w1, b1, w2, b2, w_ih, w_hh, b_ih, b_hh, gamma, beta, agg,
                  per_partition, pairs, full, rest, spare, count_cols,
                  ident, w_hi, w_lo, gate_bias, rz_bias, inv_count, gamma_b, beta_b,
                  ps_a, ps_b, ps_c, ps_d, ps_e, ps_f)
        node_part(nc, x, agg, out, blocks, last_parts,
                  ident, w_hi, w_lo, gate_bias, rz_bias, inv_count, gamma_b, beta_b,
                  ps_a, ps_b, ps_c, ps_d, ps_e, ps_f)


def edge_part(nc, x, src, dst, w1, b1, w2, b2, w_ih, w_hh, b_ih, b_hh, gamma, beta, agg,
              per_partition, pairs, full, rest, spare, count_cols,
              ident, w_hi, w_lo, gate_bias, rz_bias, inv_count, gamma_b, beta_b,
              ps_a, ps_b, ps_c, ps_d, ps_e, ps_f):
    N = x.shape[0]
    with ExitStack() as ctx:
        def sb(name, shape, dt):
            return ctx.enter_context(nc.sbuf_tensor(name, shape, dt))

        def sem(name):
            return ctx.enter_context(nc.semaphore(name))

        agg_cols = agg.shape[0] * D // P
        agg_by_p = agg.rearrange("r d -> (r d)").rearrange("(p c) -> p c", p=P)
        clears = 32
        clear_cols = agg_cols // clears
        assert clear_cols * clears == agg_cols
        zeros = sb("zeros", [P, clear_cols], F32)

        w_hh_n = sb("w_hh_n", [P, GATES, D], F32)
        w_ih_n = sb("w_ih_n", [P, GATES, D], F32)
        w1_n = sb("w1_n", [P, KD, 2 * D], F32)
        w2_n = sb("w2_n", [P, KD, D], F32)
        w2_t = sb("w2_t", [P, KD, D], F32)
        b1_c = sb("b1_c", [P, KD], F32)
        b2_b = sb("b2_b", [P, D], F32)

        src_raw = sb("src_raw", [P, per_partition], I32)
        dst_raw = sb("dst_raw", [P, per_partition], I32)
        rows_f = sb("rows_f", [P, per_partition], F32)
        gather_idx = sb("gather_idx", [P, pairs, 2 * TILES], I32)
        scatter_idx = sb("scatter_idx", [P, pairs * TILES], I32)
        key_p = sb("key_p", [P, per_partition], F32)
        key_c = sb("key_c", [P, per_partition], F32)
        key_i = sb("key_i", [P, 3, per_partition], I32)
        spare_f = sb("spare_f", [P, 1], F32)
        to_spare = sb("to_spare", [P, per_partition], F32)
        repeats = sb("repeats", [P, per_partition], F32)
        iota_c = sb("iota_c", [P, count_cols], F32)
        ones = sb("ones", [P, 1], BF16)
        earlier = sb("earlier", [P, 4, P], BF16)
        four_rows = sb("four_rows", [P, 2, 4], F32)
        same_all = sb("same_all", [P, per_partition, P], BF16)
        same_earlier = sb("same_earlier", [P, 2, 4, P], BF16)

        gidx = sb("gidx", [P, 2, 2 * TILES], I32)
        sidx = sb("sidx", [P, 2, TILES], I32)
        xe = sb("xe", [P, 2, 2 * TILES, D], F32)
        xt_hi = sb("xt_hi", [P, 2, 2 * KD, PAIR], F32R)
        xt_lo = sb("xt_lo", [P, 2, 2 * KD, PAIR], F32R)
        sig = sb("sig", [P, 2, KD, PAIR], F32)
        hid = sb("hid", [P, 2, KD, PAIR], F32)
        msg = sb("msg", [P, 2, TILES, D], F32)
        same = sb("same", [P, 2, TILES, P], F32)
        total = sb("total", [P, 2, TILES, D], F32)
        hot_p = sb("hot_p", [P, 2, TILES, P], BF16)
        hot_c = sb("hot_c", [P, 2, TILES, count_cols], BF16)
        counts = sb("counts", [P, count_cols], F32)

        xt_ps = [ps_a, ps_b]
        hid_ps, msg_ps, total_ps, count_ps = ps_c, ps_d, ps_e, ps_f
        w_ps = [ps_a[:, 0], ps_a[:, 1], ps_b[:, 0], ps_b[:, 1]]
        rows_ps = [ps_c, ps_d]
        repeats_ps = ps_e

        pool_passed = sem("pool_passed")
        zeroed_tile = sem("zeroed_tile")
        cleared = sem("cleared")
        weights_in = sem("weights_in")
        bias_in = sem("bias_in")
        edges_in = sem("edges_in")
        pads_set = sem("pads_set")
        ident_zero = sem("ident_zero")
        consts_set = sem("consts_set")
        keys = sem("keys")
        w_turned = sem("w_turned")
        w_hi_done = sem("w_hi_done")
        w_lo_done = sem("w_lo_done")
        four_copied = sem("four_copied")
        rows_spread = sem("rows_spread")
        same_set = sem("same_set")
        masked = sem("masked")
        repeats_counted = sem("repeats_counted")
        scatter_step = sem("scatter_step")
        scatter_set = sem("scatter_set")
        gidx_set = sem("gidx_set")
        gathered = [sem("gathered0"), sem("gathered1")]
        xt_turned = sem("xt_turned")
        xt_hi_set = sem("xt_hi_set")
        xt_lo_set = sem("xt_lo_set")
        hid_summed = sem("hid_summed")
        sig_set = sem("sig_set")
        hid_set = sem("hid_set")
        msg_summed = sem("msg_summed")
        msg_set = sem("msg_set")
        same_f_set = sem("same_f_set")
        hot_set = sem("hot_set")
        hot_counted = sem("hot_counted")
        total_summed = sem("total_summed")
        total_set = sem("total_set")
        added = sem("added")
        counts_set = sem("counts_set")

        chunks = [(w_hh_n, k, m) for k in range(KD) for m in range(GATES)]
        chunks += [(w_ih_n, k, m) for k in range(KD) for m in range(GATES)]
        chunks += [(w1_n, k, m) for k in range(2 * KD) for m in range(KD)]
        chunks += [(w2_n, k, m) for k in range(KD) for m in range(KD)]
        groups = [chunks[g:g + 4] for g in range(0, len(chunks), 4)]
        split_groups = W_COLS // BANK
        quads = per_partition // 4
        assert per_partition % 4 == 0 and pairs % 2 == 0 and len(groups) == split_groups + 1

        block = ctx.enter_context(nc.Block())

        @block.sync
        def _(sp):
            sp.wait_ge(pads_set, 2)
            for raw, edge in ((src_raw, src), (dst_raw, dst)):
                sp.dma_start(raw[0:full, :], edge[0:full * per_partition].rearrange(
                    "(p c) -> p c", p=full)).then_inc(edges_in, 16)
                if rest:
                    sp.dma_start(raw[full:full + 1, 0:rest], edge[full * per_partition:].rearrange(
                        "(p c) -> p c", p=1)).then_inc(edges_in, 16)
            for nat, w in ((w_hh_n, w_hh), (w_ih_n, w_ih), (w1_n, w1), (w2_n, w2)):
                sp.dma_start(nat[:], w.rearrange("(m p) k -> p m k", p=P)).then_inc(weights_in, 16)
            with nc.allow_non_contiguous_dma(reason="a few bias columns"):
                sp.dma_start(b1_c[:], b1.rearrange("(c p) -> p c", p=P)).then_inc(bias_in, 16)
                sp.dma_start(gate_bias[:, 0], b_ih.rearrange("(c p) -> p c", p=P)).then_inc(bias_in, 16)
                sp.dma_start(gate_bias[:, 1], b_hh.rearrange("(c p) -> p c", p=P)).then_inc(bias_in, 16)
            for row, v in ((b2_b, b2), (gamma_b, gamma), (beta_b, beta)):
                sp.dma_start(row[:], v.rearrange("(a d) -> a d", a=1).to_broadcast([P, D])).then_inc(bias_in, 16)
            sp.wait_ge(zeroed_tile, 1)
            with sp.Fori(0, clears) as c:
                sp.dma_start(agg_by_p[:, bass.ds(c * clear_cols, clear_cols)], zeros[:]).then_inc(cleared, 16)

        @block.gpsimd
        def _(pool):
            pool.memset(src_raw[:], spare + P - 1).then_inc(pads_set, 1)
            pool.memset(dst_raw[:], 0).then_inc(pads_set, 1)
            pool.memset(ident[:], 0.0).then_inc(ident_zero, 1)
            pool.memset(earlier[:], 1.0).then_inc(ident_zero, 1)
            pool.memset(ones[:], 1.0).then_inc(consts_set, 1)
            pool.wait_ge(ident_zero, 2)
            pool.affine_select(out=ident[:], in_=ident[:], compare_op=ALU.not_equal, fill=1.0, base=0,
                               pattern=[[-1, P]], channel_multiplier=1).then_inc(consts_set, 1)
            pool.affine_select(out=earlier[:], in_=earlier[:], compare_op=ALU.is_gt, fill=0.0, base=0,
                               pattern=[[0, 4], [1, P]], channel_multiplier=-1).then_inc(consts_set, 1)
            pool.iota(spare_f[:], [[0, 1]], base=spare, channel_multiplier=1,
                      allow_small_or_imprecise_dtypes=True).then_inc(consts_set, 1)
            pool.iota(iota_c[:], [[1, count_cols]], base=0, channel_multiplier=0,
                      allow_small_or_imprecise_dtypes=True).then_inc(consts_set, 1)

            gate = Gate(pool, pool_passed)

            def gather(t):
                pool.wait_ge(gidx_set, t.n + 1)
                if not (isinstance(t.n, int) and t.n < 2):
                    pool.wait_ge(xt_turned, t.n - 1)
                gate.take_waits()
                for j in range(2 * TILES):
                    pool.indirect_dma_start(
                        out=xe[:, t.slot, j, :], out_offset=None, in_=x[:, :],
                        in_offset=bass.IndirectOffsetOnAxis(ap=gidx[:, t.slot, j:j + 1], axis=0),
                    ).then_inc(gathered[t.slot], 16)

            def add(t):
                for j in range(TILES):
                    if j == 0:
                        pool.wait_ge(total_set, 2 * (t.n + 1))
                    pool.wait_ge(added, 16 * (TILES * t.n + j))
                    gate.take_waits()
                    pool.indirect_dma_start(
                        out=agg[:, :], in_=total[:, t.slot, j, :], in_offset=None,
                        out_offset=bass.IndirectOffsetOnAxis(ap=sidx[:, t.slot, j:j + 1], axis=0),
                        compute_op=ALU.add,
                    ).then_inc(added, 16)

            LAG = 5

            def step(t, peeled):
                if peeled is None or peeled < pairs:
                    gather(t)
                if peeled is None or peeled >= LAG:
                    if peeled == LAG:
                        pool.wait_ge(cleared, 16 * clears)
                    add(t.at(-LAG))

            for c in range(LAG + 1):
                step(Turn(0, c), peeled=c)
            rounds = (pairs - LAG - 1) // 2
            with pool.Fori(0, rounds) as i:
                for c in range(2):
                    step(Turn(i, LAG + 1 + c), peeled=None)
            for c in range(LAG + 1 + 2 * rounds, pairs + LAG):
                step(Turn(0, c), peeled=c)
            pool.wait_ge(added, 16 * TILES * pairs)

        @block.scalar
        def _(act):
            for g, group in enumerate(groups):
                act.wait_ge(w_turned, g + 1)
                if g < split_groups:
                    act.copy(w_hi[:, g * BANK:(g + 1) * BANK], w_ps[g % 4]).then_inc(w_hi_done, 1)
                else:
                    act.copy(w2_t[:].rearrange("p k d -> p (k d)"), w_ps[g % 4]).then_inc(w_hi_done, 1)
            act.wait_ge(bias_in, 96)

            def split_x(t):
                act.wait_ge(xt_turned, t.n + 1)
                if not (isinstance(t.n, int) and t.n < 2):
                    act.wait_ge(hid_summed, t.n - 1)
                act.copy(xt_hi[:, t.slot].rearrange("p k e -> p (k e)"),
                         xt_ps[t.slot][:].rearrange("p k e -> p (k e)")).then_inc(xt_hi_set, 1)

            def step(t, peeled):
                first = peeled == 0
                if first:
                    split_x(t)
                if peeled is None or peeled + 1 < pairs:
                    split_x(t.at(1))
                if peeled is None or peeled < pairs:
                    act.wait_ge(hid_summed, t.n + 1)
                    if peeled is None or peeled >= 2:
                        act.wait_ge(hid_set, t.n - 1)
                    for m in range(KD):
                        ins = act.activation(sig[:, t.slot, m], hid_ps[:, m * PAIR:(m + 1) * PAIR],
                                             ACT.Sigmoid, bias=b1_c[:, m:m + 1])
                    ins.then_inc(sig_set, 1)
                    if peeled == 0:
                        act.wait_ge(scatter_set, 1)
                    if peeled is None or peeled >= 2:
                        act.wait_ge(total_summed, t.n - 1)
                    act.copy(same[:, t.slot].rearrange("p t e -> p (t e)"),
                             same_all[:, bass.ds(t.n * TILES, TILES), :].rearrange("p t e -> p (t e)")
                             ).then_inc(same_f_set, 1)
                if peeled is None or peeled >= 2:
                    u = t.at(-2)
                    act.wait_ge(total_summed, u.n + 1)
                    if peeled is None or peeled >= 4:
                        act.wait_ge(added, 16 * TILES * (u.n - 1))
                    act.copy(sidx[:, u.slot], scatter_idx[:, bass.ds(u.n * TILES, TILES)]).then_inc(total_set, 1)
                    act.copy(total[:, u.slot].rearrange("p t d -> p (t d)"), total_ps[:]).then_inc(total_set, 1)

            turns_lead4(act, pairs, step)

        @block.tensor
        def _(pe):
            pe.wait_ge(consts_set, 5)
            pe.wait_ge(weights_in, 64)
            for g, group in enumerate(groups):
                if g >= 4:
                    pe.wait_ge(w_hi_done, g - 3)
                    pe.wait_ge(w_lo_done, g - 3)
                for c, (nat, k, m) in enumerate(group):
                    ins = pe.transpose(w_ps[g % 4][:, c * P:(c + 1) * P], nat[:, m, k * P:(k + 1) * P], ident[:])
                ins.then_inc(w_turned, 1)

            def spread(t):
                pe.wait_ge(four_copied, t.n + 1)
                if not (isinstance(t.n, int) and t.n < 2):
                    pe.wait_ge(same_set, t.n - 1)
                for j in range(4):
                    ins = pe.transpose(rows_ps[t.slot][:, j * P:(j + 1) * P],
                                       four_rows[:, t.slot, j:j + 1].to_broadcast([P, P]), ident[:])
                ins.then_inc(rows_spread, 1)

            def count_repeats(t):
                pe.wait_ge(masked, t.n + 1)
                for j in range(4):
                    ins = pe.matmul(repeats_ps[:, bass.ds(t.n * 4 + j, 1)], same_earlier[:, t.slot, j],
                                    ones[:], start=True, stop=True)
                ins.then_inc(repeats_counted, 1)

            def leader_step(t, peeled):
                if peeled is None or peeled < quads:
                    spread(t)
                if peeled is None or peeled >= 1:
                    count_repeats(t.at(-1))

            leader_turns(pe, quads, leader_step)

            def turn_x(t):
                pe.wait_ge(gathered[t.slot], 64 * (t.use + 1))
                if not (isinstance(t.n, int) and t.n < 2):
                    pe.wait_ge(xt_hi_set, t.n - 1)
                    pe.wait_ge(xt_lo_set, t.n - 1)
                for e in range(TILES):
                    for k in range(2 * KD):
                        ins = pe.transpose(
                            xt_ps[t.slot][:].rearrange("p a (b e) -> p (a b) e", b=2)[:, k, e * P:(e + 1) * P],
                            xe[:, t.slot, 2 * e + k // KD, (k % KD) * P:(k % KD + 1) * P], ident[:])
                ins.then_inc(xt_turned, 1)

            def hidden(t, peeled):
                pe.wait_ge(xt_hi_set, t.n + 1)
                pe.wait_ge(xt_lo_set, t.n + 1)
                if peeled is None or peeled >= 1:
                    pe.wait_ge(hid_set, t.n)
                for m in range(KD):
                    acc = hid_ps[:, m * PAIR:(m + 1) * PAIR]
                    for k in range(2 * KD):
                        cols = slice(W1C + (k * KD + m) * P, W1C + (k * KD + m + 1) * P)
                        pe.matmul(acc, w_hi[:, cols], xt_hi[:, t.slot, k], start=(k == 0), stop=False)
                        pe.matmul(acc, w_hi[:, cols], xt_lo[:, t.slot, k], start=False, stop=False)
                        ins = pe.matmul(acc, w_lo[:, cols], xt_hi[:, t.slot, k], start=False,
                                        stop=(k == 2 * KD - 1))
                ins.then_inc(hid_summed, 1)

            def count(t, peeled):
                pe.wait_ge(hot_set, t.n + 1)
                for j in range(TILES):
                    ins = pe.matmul(count_ps[:, 0:count_cols], hot_p[:, t.slot, j], hot_c[:, t.slot, j],
                                    start=(peeled == 0 and j == 0),
                                    stop=(peeled == pairs - 1 and j == TILES - 1), skip_group_check=True)
                ins.then_inc(hot_counted, 1)

            def message(t, peeled):
                pe.wait_ge(hid_set, t.n + 1)
                if peeled is None or peeled >= 2:
                    pe.wait_ge(msg_set, t.n)
                for j in range(TILES):
                    for k in range(KD):
                        ins = pe.matmul(msg_ps[:, j * D:(j + 1) * D], hid[:, t.slot, k, j * P:(j + 1) * P],
                                        w2_t[:, k], start=(k == 0), stop=(k == KD - 1))
                ins.then_inc(msg_summed, 1)

            def sums(t, peeled):
                pe.wait_ge(msg_set, t.n + 1)
                pe.wait_ge(same_f_set, t.n + 1)
                if peeled is None or peeled >= 3:
                    pe.wait_ge(total_set, 2 * t.n)
                for j in range(TILES):
                    ins = pe.matmul(total_ps[:, j * D:(j + 1) * D], same[:, t.slot, j], msg[:, t.slot, j],
                                    start=True, stop=True)
                ins.then_inc(total_summed, 1)

            def step(t, peeled):
                if peeled == 0:
                    pe.wait_ge(w_hi_done, len(groups))
                    pe.wait_ge(w_lo_done, split_groups)
                    turn_x(t)
                if peeled is None or peeled + 1 < pairs:
                    turn_x(t.at(1))
                if peeled is None or peeled < pairs:
                    if peeled == 0:
                        pe.wait_ge(scatter_set, 1)
                    hidden(t, peeled)
                    count(t, peeled)
                if peeled is None or 1 <= peeled <= pairs:
                    message(t.at(-1), peeled)
                if peeled is None or peeled >= 2:
                    sums(t.at(-2), peeled)

            turns_lead4(pe, pairs, step)

        @block.vector
        def _(dve):
            dve.memset(zeros[:], 0.0).then_inc(zeroed_tile, 1)

            dve.wait_ge(edges_in, 64 if rest else 32)
            g4 = gather_idx[:].rearrange("p q (t s) -> p q t s", s=2)
            as_pairs = lambda a: a.rearrange("p (q t) -> p q t", t=TILES)
            dve.tensor_scalar(g4[:, :, :, 0], as_pairs(src_raw[:]), float(N - 1), None, ALU.min).then_inc(keys, 1)
            dve.tensor_copy(g4[:, :, :, 1], as_pairs(dst_raw[:])).then_inc(keys, 1)
            dve.wait_ge(keys, 2)

            def copy_gidx(t):
                dve.tensor_copy(gidx[:, t.slot], gather_idx[:, bass.ds(t.n, 1), :].rearrange(
                    "p q j -> p (q j)")).then_inc(gidx_set, 1)

            copy_gidx(Turn(0, 0))
            copy_gidx(Turn(0, 1))
            dve.tensor_copy(rows_f[:], src_raw[:]).then_inc(keys, 1)
            dve.tensor_scalar(key_i[:, 0], src_raw[:], 2, P - 1, ALU.logical_shift_right,
                              ALU.bitwise_and).then_inc(keys, 1)
            dve.tensor_scalar(key_i[:, 1], src_raw[:], 9, 2, ALU.logical_shift_right,
                              ALU.logical_shift_left).then_inc(keys, 1)
            dve.tensor_scalar(key_i[:, 2], src_raw[:], ROWS - 1, None, ALU.bitwise_and).then_inc(keys, 1)
            dve.wait_ge(keys, 6)
            dve.tensor_copy(key_p[:], key_i[:, 0]).then_inc(keys, 1)
            dve.tensor_tensor(key_c[:], key_i[:, 1], key_i[:, 2], ALU.add).then_inc(keys, 1)
            dve.wait_ge(keys, 8)

            for g in range(split_groups):
                dve.wait_ge(w_hi_done, g + 1)
                cols = slice(g * BANK, (g + 1) * BANK)
                dve.tensor_tensor(w_lo[:, cols], w_ps[g % 4], w_hi[:, cols].bitcast(F32),
                                  ALU.subtract).then_inc(w_lo_done, 1)
            dve.wait_ge(consts_set, 5)

            def copy_rows(t):
                if not (isinstance(t.n, int) and t.n < 2):
                    dve.wait_ge(rows_spread, t.n - 1)
                dve.tensor_copy(four_rows[:, t.slot], rows_f[:, bass.ds(t.n * 4, 4)]).then_inc(four_copied, 1)

            def compare(t):
                dve.wait_ge(rows_spread, t.n + 1)
                four = same_all[:, bass.ds(t.n * 4, 4), :]
                dve.tensor_tensor(four, rows_ps[t.slot][:].rearrange("p (t e) -> p t e", t=4),
                                  rows_f[:, bass.ds(t.n * 4, 4)].unsqueeze(2).to_broadcast([P, 4, P]),
                                  ALU.is_equal).then_inc(same_set, 1)
                dve.wait_ge(same_set, t.n + 1)
                if not (isinstance(t.n, int) and t.n < 2):
                    dve.wait_ge(repeats_counted, t.n - 1)
                dve.tensor_tensor(same_earlier[:, t.slot], four, earlier[:], ALU.mult).then_inc(masked, 1)

            def leader_step(t, peeled):
                if peeled is None or peeled < quads:
                    copy_rows(t)
                if peeled is None or peeled >= 1:
                    compare(t.at(-1))

            leader_turns(dve, quads, leader_step)

            dve.wait_ge(repeats_counted, quads)
            dve.tensor_scalar(repeats[:], repeats_ps[:, 0:per_partition], 1.0, None, ALU.min).then_inc(scatter_step, 1)
            dve.tensor_scalar(to_spare[:], rows_f[:], -1.0, spare_f[:, 0:1], ALU.mult, ALU.add).then_inc(scatter_step, 1)
            dve.wait_ge(scatter_step, 2)
            dve.tensor_tensor(repeats[:], repeats[:], to_spare[:], ALU.mult).then_inc(scatter_step, 1)
            dve.wait_ge(scatter_step, 3)
            dve.tensor_tensor(scatter_idx[:], repeats[:], rows_f[:], ALU.add).then_inc(scatter_set, 1)
            dve.wait_ge(bias_in, 96)
            dve.tensor_tensor(rz_bias[:], gate_bias[:, 0, 0:2 * KD], gate_bias[:, 1, 0:2 * KD],
                              ALU.add).then_inc(scatter_step, 1)

            def low_x(t):
                dve.wait_ge(xt_hi_set, t.n + 1)
                if not (isinstance(t.n, int) and t.n < 2):
                    dve.wait_ge(hid_summed, t.n - 1)
                dve.tensor_tensor(xt_lo[:, t.slot].rearrange("p k e -> p (k e)"),
                                  xt_ps[t.slot][:].rearrange("p k e -> p (k e)"),
                                  xt_hi[:, t.slot].rearrange("p k e -> p (k e)").bitcast(F32),
                                  ALU.subtract).then_inc(xt_lo_set, 1)

            def step(t, peeled):
                if peeled == 0:
                    low_x(t)
                if peeled is None or peeled + 1 < pairs:
                    low_x(t.at(1))
                if peeled is None or peeled < pairs:
                    if peeled is None or peeled + 2 < pairs:
                        dve.wait_ge(xt_turned, t.n + 1)
                        copy_gidx(t.at(2))
                    if peeled is None or peeled >= 2:
                        dve.wait_ge(hot_counted, t.n - 1)
                    for j in range(TILES):
                        dve.tensor_scalar(hot_p[:, t.slot, j], iota_c[:, 0:P], key_p[:, bass.ds(t.n * TILES + j, 1)],
                                          None, ALU.is_equal)
                        ins = dve.tensor_scalar(hot_c[:, t.slot, j], iota_c[:],
                                                key_c[:, bass.ds(t.n * TILES + j, 1)], None, ALU.is_equal)
                    ins.then_inc(hot_set, 1)
                    dve.wait_ge(sig_set, t.n + 1)
                    if peeled is None or peeled >= 2:
                        dve.wait_ge(msg_summed, t.n - 1)
                    for m in range(KD):
                        ins = dve.scalar_tensor_tensor(
                            out=hid[:, t.slot, m], in0=hid_ps[:, m * PAIR:(m + 1) * PAIR], scalar=b1_c[:, m:m + 1],
                            in1=sig[:, t.slot, m], op0=ALU.add, op1=ALU.mult)
                    ins.then_inc(hid_set, 1)
                if peeled is None or 1 <= peeled <= pairs:
                    u = t.at(-1)
                    dve.wait_ge(msg_summed, u.n + 1)
                    if peeled is None or peeled >= 3:
                        dve.wait_ge(total_summed, u.n - 1)
                    dve.tensor_tensor(msg[:, u.slot], msg_ps[:].rearrange("p (t d) -> p t d", t=TILES),
                                      b2_b[:].unsqueeze(1).to_broadcast([P, TILES, D]), ALU.add).then_inc(msg_set, 1)

            turns_lead4(dve, pairs, step)

            dve.wait_ge(hot_counted, pairs)
            dve.tensor_scalar(counts[:], count_ps[:, 0:count_cols], EPS_COUNT, None, ALU.add).then_inc(counts_set, 1)
            dve.wait_ge(counts_set, 1)
            dve.reciprocal(inv_count[:], counts[:]).then_inc(counts_set, 1)


def turns_lead4(engine, total, step):
    for c in range(4):
        step(Turn(0, c), peeled=c)
    rounds = (total - 2 - 4) // 2
    with engine.Fori(0, rounds) as i:
        for c in range(2):
            step(Turn(i, 4 + c), peeled=None)
    for c in range(4 + 2 * rounds, total + 2):
        step(Turn(0, c), peeled=c)


def leader_turns(engine, total, step):
    for c in range(3):
        step(Turn(0, c), peeled=c)
    rounds = (total - 1 - 3) // 2
    with engine.Fori(0, rounds) as i:
        for c in range(2):
            step(Turn(i, 3 + c), peeled=None)
    for c in range(3 + 2 * rounds, total + 1):
        step(Turn(0, c), peeled=c)


def node_part(nc, x, agg, out, blocks, last_parts,
              ident, w_hi, w_lo, gate_bias, rz_bias, inv_count, gamma_b, beta_b,
              ps_a, ps_b, ps_c, ps_d, ps_e, ps_f):
    with ExitStack() as ctx:
        def sb(name, shape, dt):
            return ctx.enter_context(nc.sbuf_tensor(name, shape, dt))

        def sem(name):
            return ctx.enter_context(nc.semaphore(name))

        x_in = sb("x_in", [P, 2, ROWS, D], F32)
        a_in = sb("a_in", [P, 2, ROWS, D], F32)
        mean = sb("mean", [P, 2, ROWS, D], F32)
        x_beta = sb("x_beta", [P, 2, ROWS, D], F32)
        scaled = sb("scaled", [P, ROWS, D], F32)
        resid = sb("resid", [P, 2, ROWS, D], F32)
        result = sb("result", [P, 2, ROWS, D], F32)
        xt = sb("xt", [P, 2, KD, BLOCK], F32)
        xt_hi = sb("nxt_hi", [P, 2, KD, BLOCK], F32R)
        xt_lo = sb("nxt_lo", [P, 2, KD, BLOCK], F32R)
        at_hi = sb("at_hi", [P, 2, KD, BLOCK], F32R)
        at_lo = sb("at_lo", [P, 2, KD, BLOCK], F32R)
        r = sb("r", [P, KD, BLOCK], F32)
        z = sb("z", [P, KD, BLOCK], F32)
        pre = sb("pre", [P, KD, BLOCK], F32)
        cand = sb("cand", [P, KD, BLOCK], F32)
        diff = sb("diff", [P, KD, BLOCK], F32)
        new = sb("new", [P, KD, BLOCK], F32)
        stats = sb("stats", [P, 2, ROWS, 6], F32)
        norm = sb("norm", [P, 2, ROWS, 2], F32)
        var_eps = sb("var_eps", [P, 2, ROWS], F32)
        rstd = sb("rstd", [P, 2, ROWS], F32)
        shift = sb("shift", [P, ROWS], F32)
        minus_half = sb("minus_half", [P, ROWS], F32)

        turn_ps, back_ps = ps_a, ps_b
        r_ps, z_ps, h_ps, i_ps = ps_c, ps_d, ps_e, ps_f

        x_landed = [sem("x_landed0"), sem("x_landed1")]
        a_landed = [sem("a_landed0"), sem("a_landed1")]
        stored = [sem("stored0"), sem("stored1")]
        dve_passed = sem("dve_passed")
        half_set = sem("half_set")
        mean_set = sem("mean_set")
        x_beta_set = sem("x_beta_set")
        x_turned = sem("x_turned")
        a_turned = sem("a_turned")
        xt_set = sem("xt_set")
        xt_hi_set = sem("nxt_hi_set")
        xt_lo_set = sem("nxt_lo_set")
        at_hi_set = sem("at_hi_set")
        at_lo_set = sem("at_lo_set")
        r_summed = sem("r_summed")
        z_summed = sem("z_summed")
        h_summed = sem("h_summed")
        i_summed = sem("i_summed")
        r_set = sem("r_set")
        z_set = sem("z_set")
        rh_set = sem("rh_set")
        pre_set = sem("pre_set")
        cand_set = sem("cand_set")
        diff_set = sem("diff_set")
        zdiff_set = sem("zdiff_set")
        new_set = sem("new_set")
        new_turned = sem("new_turned")
        stats1_set = sem("stats1_set")
        norm1_set = sem("norm1_set")
        var1_set = sem("var1_set")
        rstd1_set = sem("rstd1_set")
        scaled_set = sem("scaled_set")
        resid_set = sem("resid_set")
        stats2_set = sem("stats2_set")
        norm2_set = sem("norm2_set")
        var2_set = sem("var2_set")
        rstd2_set = sem("rstd2_set")
        shift_set = sem("shift_set")
        result_set = sem("result_set")

        def rows_of(a, n, parts=P):
            return a[bass.ds(n * BLOCK, parts * ROWS), :].rearrange("(p j) d -> p j d", j=ROWS)

        def steps(engine, step):
            for c in range(3):
                step(Turn(0, c), peeled=c)
            rounds = (blocks - 3 - 3) // 2
            with engine.Fori(0, rounds) as i:
                for c in range(2):
                    step(Turn(i, 3 + c), peeled=None)
            for c in range(3 + 2 * rounds, blocks + 1):
                step(Turn(0, c), peeled=c)

        def gates(peeled):
            return peeled is None or peeled < blocks

        def turns_next(peeled):
            return peeled is None or peeled + 1 < blocks

        def norms(peeled):
            return peeled is None or peeled >= 1

        block = ctx.enter_context(nc.Block())

        @block.sync
        def _(sp):
            def load(t, parts):
                if not (isinstance(t.n, int) and t.n < 2):
                    sp.wait_ge(x_turned, t.n - 1)
                    sp.wait_ge(x_beta_set, t.n - 1)
                sp.dma_start(x_in[0:parts, t.slot], rows_of(x, t.n, parts)).then_inc(x_landed[t.slot], 16)
                if not (isinstance(t.n, int) and t.n < 2):
                    sp.wait_ge(mean_set, t.n - 1)
                sp.dma_start(a_in[0:parts, t.slot], rows_of(agg, t.n, parts)).then_inc(a_landed[t.slot], 16)

            def store(t, parts):
                sp.wait_ge(result_set, t.n + 1)
                sp.dma_start(rows_of(out, t.n, parts), result[0:parts, t.slot]).then_inc(stored[t.slot], 16)

            def step(t, peeled):
                if peeled == 0:
                    load(t, P)
                    load(t.at(1), P)
                if peeled is None or peeled + 2 < blocks:
                    load(t.at(2), last_parts if peeled == blocks - 3 else P)
                if norms(peeled):
                    store(t.at(-1), last_parts if peeled == blocks else P)

            steps(sp, step)
            sp.wait_ge(stored[0], 16 * ((blocks + 1) // 2))
            sp.wait_ge(stored[1], 16 * (blocks // 2))

        @block.gpsimd
        def _(pool):
            pool.memset(minus_half[:], -0.5).then_inc(half_set, 1)
            pool.wait_ge(half_set, 1)

            def prepare(t):
                pool.wait_ge(a_landed[t.slot], 16 * (t.use + 1))
                if not (isinstance(t.n, int) and t.n < 2):
                    pool.wait_ge(a_turned, t.n - 1)
                pool.tensor_tensor(mean[:, t.slot], a_in[:, t.slot],
                                   inv_count[:, bass.ds(t.n * ROWS, ROWS)].unsqueeze(2).to_broadcast([P, ROWS, D]),
                                   ALU.mult).then_inc(mean_set, 1)

            def add_beta(t):
                pool.wait_ge(x_landed[t.slot], 16 * (t.use + 1))
                if not (isinstance(t.n, int) and t.n < 2):
                    pool.wait_ge(resid_set, t.n - 1)
                pool.tensor_tensor(x_beta[:, t.slot], x_in[:, t.slot],
                                   beta_b[:].unsqueeze(1).to_broadcast([P, ROWS, D]), ALU.add).then_inc(x_beta_set, 1)

            def difference(t, h, peeled):
                pool.wait_ge(cand_set, 2 * t.n + h + 1)
                if peeled is None or peeled >= 1:
                    pool.wait_ge(zdiff_set, 2 * t.n + h - 1)
                pool.tensor_tensor(diff[:, h], xt[:, t.slot, h], cand[:, h], ALU.subtract).then_inc(diff_set, 1)

            def root(t, which, var_set, rstd_set):
                pool.wait_ge(var_set, t.n + 1)
                pool.tensor_tensor(rstd[:, which], var_eps[:, which], minus_half[:], ALU.pow).then_inc(rstd_set, 1)

            def step(t, peeled):
                if peeled == 0:
                    prepare(t)
                    add_beta(t)
                if turns_next(peeled):
                    prepare(t.at(1))
                if norms(peeled):
                    root(t.at(-1), 0, var1_set, rstd1_set)
                if gates(peeled):
                    difference(t, 0, peeled)
                if norms(peeled):
                    root(t.at(-1), 1, var2_set, rstd2_set)
                if turns_next(peeled):
                    add_beta(t.at(1))
                if gates(peeled):
                    difference(t, 1, peeled)

            steps(pool, step)

        @block.scalar
        def _(act):
            def split(t, src_sem, dst, dst_sem, peeled_first):
                act.wait_ge(src_sem, t.n + 1)
                if not (isinstance(t.n, int) and t.n < 2):
                    act.wait_ge(i_summed, 2 * (t.n - 1))
                act.copy(dst[:, t.slot].rearrange("p k n -> p (k n)"),
                         turn_ps[:].rearrange("p k n -> p (k n)")).then_inc(dst_sem, 1)

            def keep_x(t):
                if not (isinstance(t.n, int) and t.n < 2):
                    act.wait_ge(diff_set, 2 * (t.n - 1))
                act.copy(xt[:, t.slot].rearrange("p k n -> p (k n)"),
                         turn_ps[:].rearrange("p k n -> p (k n)")).then_inc(xt_set, 1)

            def sigmoids(t, h, peeled):
                act.wait_ge(r_summed, 2 * t.n + h + 1)
                if peeled is None or peeled >= 1:
                    act.wait_ge(rh_set, 2 * t.n + h - 1)
                act.activation(r[:, h], r_ps[:], ACT.Sigmoid, bias=rz_bias[:, h:h + 1]).then_inc(r_set, 1)
                act.wait_ge(z_summed, 2 * t.n + h + 1)
                if peeled is None or peeled >= 1:
                    act.wait_ge(zdiff_set, 2 * t.n + h - 1)
                act.activation(z[:, h], z_ps[:], ACT.Sigmoid, bias=rz_bias[:, KD + h:KD + h + 1]).then_inc(z_set, 1)

            def tanh(t, h, peeled):
                act.wait_ge(pre_set, 2 * t.n + h + 1)
                if peeled is None or peeled >= 1:
                    act.wait_ge(new_set, 2 * t.n + h - 1)
                act.activation(cand[:, h], pre[:, h], ACT.Tanh,
                               bias=gate_bias[:, 0, 2 * KD + h:2 * KD + h + 1]).then_inc(cand_set, 1)

            def normalise(t, peeled):
                act.wait_ge(shift_set, t.n + 1)
                if peeled is None or peeled >= 3:
                    act.wait_ge(stored[t.slot], 16 * t.use)
                for j in range(ROWS):
                    ins = act.activation(result[:, t.slot, j], resid[:, t.slot, j], ACT.Identity,
                                         bias=shift[:, j:j + 1], scale=rstd[:, 1, j:j + 1])
                ins.then_inc(result_set, 1)

            def step(t, peeled):
                if peeled == 0:
                    split(t, x_turned, xt_hi, xt_hi_set, True)
                    keep_x(t)
                    split(t, a_turned, at_hi, at_hi_set, True)
                if gates(peeled):
                    sigmoids(t, 0, peeled)
                if turns_next(peeled):
                    split(t.at(1), x_turned, xt_hi, xt_hi_set, False)
                    keep_x(t.at(1))
                if gates(peeled):
                    tanh(t, 0, peeled)
                    sigmoids(t, 1, peeled)
                if norms(peeled):
                    normalise(t.at(-1), peeled)
                if turns_next(peeled):
                    split(t.at(1), a_turned, at_hi, at_hi_set, False)
                if gates(peeled):
                    tanh(t, 1, peeled)

            steps(act, step)

        @block.tensor
        def _(pe):
            def turn(rows, t, done):
                for j in range(ROWS):
                    for k in range(KD):
                        ins = pe.transpose(turn_ps[:, k, j * P:(j + 1) * P], rows[:, t.slot, j, k * P:(k + 1) * P],
                                           ident[:])
                ins.then_inc(done, 1)

            def turn_x(t):
                pe.wait_ge(x_landed[t.slot], 16 * (t.use + 1))
                if not (isinstance(t.n, int) and t.n < 1):
                    pe.wait_ge(at_hi_set, t.n)
                    pe.wait_ge(at_lo_set, t.n)
                turn(x_in, t, x_turned)

            def turn_mean(t):
                pe.wait_ge(mean_set, t.n + 1)
                pe.wait_ge(xt_set, t.n + 1)
                pe.wait_ge(xt_lo_set, t.n + 1)
                turn(mean, t, a_turned)

            def products(acc, base, chunk, hi, lo, slot, start, stop):
                for k in range(KD):
                    cols = slice(base + (k * GATES + chunk) * P, base + (k * GATES + chunk + 1) * P)
                    pe.matmul(acc, w_hi[:, cols], hi[:, slot, k], start=(start and k == 0), stop=False)
                    pe.matmul(acc, w_hi[:, cols], lo[:, slot, k], start=False, stop=False)
                    ins = pe.matmul(acc, w_lo[:, cols], hi[:, slot, k], start=False, stop=(stop and k == KD - 1))
                return ins

            def gate_sums(t, h, peeled):
                later = peeled is None or peeled >= 1 or h == 1
                if h == 0:
                    pe.wait_ge(xt_hi_set, t.n + 1)
                    pe.wait_ge(xt_lo_set, t.n + 1)
                if later:
                    pe.wait_ge(r_set, 2 * t.n + h)
                products(r_ps[:], HH, h, xt_hi, xt_lo, t.slot, True, False)
                if h == 0:
                    pe.wait_ge(at_hi_set, t.n + 1)
                    pe.wait_ge(at_lo_set, t.n + 1)
                products(r_ps[:], IH, h, at_hi, at_lo, t.slot, False, True).then_inc(r_summed, 1)
                if later:
                    pe.wait_ge(z_set, 2 * t.n + h)
                products(z_ps[:], HH, KD + h, xt_hi, xt_lo, t.slot, True, False)
                products(z_ps[:], IH, KD + h, at_hi, at_lo, t.slot, False, True).then_inc(z_summed, 1)
                if later:
                    pe.wait_ge(rh_set, 2 * t.n + h)
                products(h_ps[:], HH, 2 * KD + h, xt_hi, xt_lo, t.slot, True, True).then_inc(h_summed, 1)
                if later:
                    pe.wait_ge(pre_set, 2 * t.n + h)
                products(i_ps[:], IH, 2 * KD + h, at_hi, at_lo, t.slot, True, True).then_inc(i_summed, 1)

            def turn_back(t, h, peeled):
                pe.wait_ge(new_set, 2 * t.n + h + 1)
                if h == 0 and (peeled is None or peeled >= 1):
                    pe.wait_ge(scaled_set, ROWS * t.n)
                for j in range(ROWS):
                    ins = pe.transpose(back_ps[:].rearrange("p a (b d) -> p (a b) d", d=D)[:, j, h * P:(h + 1) * P],
                                       new[:, h, j * P:(j + 1) * P], ident[:])
                ins.then_inc(new_turned, 1)

            def step(t, peeled):
                if peeled == 0:
                    turn_x(t)
                    turn_mean(t)
                if gates(peeled):
                    gate_sums(t, 0, peeled)
                if norms(peeled):
                    turn_back(t.at(-1), 1, peeled)
                if turns_next(peeled):
                    turn_x(t.at(1))
                if gates(peeled):
                    gate_sums(t, 1, peeled)
                if turns_next(peeled):
                    turn_mean(t.at(1))
                if gates(peeled):
                    turn_back(t, 0, peeled)

            steps(pe, step)

        @block.vector
        def _(dve):
            gate = Gate(dve, dve_passed)
            back = back_ps[:].rearrange("p a (b d) -> p (a b) d", d=D)

            def low(t, hi, lo, bank_free, lo_set):
                dve.wait_ge(bank_free, t.n + 1)
                dve.tensor_tensor(lo[:, t.slot].rearrange("p k n -> p (k n)"),
                                  turn_ps[:].rearrange("p k n -> p (k n)"),
                                  hi[:, t.slot].rearrange("p k n -> p (k n)").bitcast(F32),
                                  ALU.subtract).then_inc(lo_set, 1)

            def candidate(t, h, peeled):
                dve.wait_ge(r_set, 2 * t.n + h + 1)
                dve.wait_ge(h_summed, 2 * t.n + h + 1)
                if peeled is None or peeled >= 1:
                    dve.wait_ge(cand_set, 2 * t.n + h - 1)
                dve.scalar_tensor_tensor(out=pre[:, h], in0=h_ps[:],
                                         scalar=gate_bias[:, 1, 2 * KD + h:2 * KD + h + 1], in1=r[:, h],
                                         op0=ALU.add, op1=ALU.mult).then_inc(rh_set, 1)
                dve.wait_ge(i_summed, 2 * t.n + h + 1)
                dve.wait_ge(rh_set, 2 * t.n + h + 1)
                dve.tensor_tensor(pre[:, h], i_ps[:], pre[:, h], ALU.add).then_inc(pre_set, 1)

            def update(t, h, peeled):
                dve.wait_ge(diff_set, 2 * t.n + h + 1)
                dve.wait_ge(z_set, 2 * t.n + h + 1)
                if peeled is None or peeled >= 1:
                    dve.wait_ge(new_turned, 2 * t.n + h - 1)
                dve.tensor_tensor(new[:, h], diff[:, h], z[:, h], ALU.mult).then_inc(zdiff_set, 1)
                dve.wait_ge(zdiff_set, 2 * t.n + h + 1)
                dve.tensor_tensor(new[:, h], new[:, h], cand[:, h], ALU.add).then_inc(new_set, 1)

            def statistics(t, which, rows, stats_set, norm_set, var_set):
                for j in range(ROWS):
                    dve.bn_stats(stats[:, which, j], rows[j]).then_inc(stats_set, 1)
                dve.wait_ge(stats_set, ROWS * (t.n + 1))
                gate.take_waits()
                for j in range(ROWS):
                    dve.bn_aggr(norm[:, which, j], stats[:, which, j]).then_inc(norm_set, 1)
                dve.wait_ge(norm_set, ROWS * (t.n + 1))
                dve.tensor_scalar(var_eps[:, which], norm[:, which, :, 1], EPS_NORM, None, ALU.add).then_inc(var_set, 1)

            def residual(t, peeled):
                for j in range(ROWS):
                    dve.scalar_tensor_tensor(out=scaled[:, j], in0=back[:, j], scalar=norm[:, 0, j, 0:1],
                                             in1=gamma_b[:], op0=ALU.subtract, op1=ALU.mult).then_inc(scaled_set, 1)
                dve.wait_ge(rstd1_set, t.n + 1)
                dve.wait_ge(x_beta_set, t.n + 1)
                if peeled is None or peeled >= 3:
                    dve.wait_ge(result_set, t.n - 1)
                for j in range(ROWS):
                    dve.wait_ge(scaled_set, ROWS * t.n + j + 1)
                    ins = dve.scalar_tensor_tensor(out=resid[:, t.slot, j], in0=scaled[:, j], scalar=rstd[:, 0, j:j + 1],
                                                   in1=x_beta[:, t.slot, j], op0=ALU.mult, op1=ALU.add)
                ins.then_inc(resid_set, 1)

            def step(t, peeled):
                if peeled == 0:
                    low(t, xt_hi, xt_lo, xt_set, xt_lo_set)
                    low(t, at_hi, at_lo, at_hi_set, at_lo_set)
                if gates(peeled):
                    candidate(t, 0, peeled)
                if turns_next(peeled):
                    low(t.at(1), xt_hi, xt_lo, xt_set, xt_lo_set)
                if norms(peeled):
                    u = t.at(-1)
                    dve.wait_ge(new_turned, 2 * (u.n + 1))
                    statistics(u, 0, [back[:, j] for j in range(ROWS)], stats1_set, norm1_set, var1_set)
                if gates(peeled):
                    update(t, 0, peeled)
                if norms(peeled):
                    u = t.at(-1)
                    residual(u, peeled)
                    dve.wait_ge(resid_set, u.n + 1)
                    statistics(u, 1, [resid[:, u.slot, j] for j in range(ROWS)], stats2_set, norm2_set, var2_set)
                if gates(peeled):
                    candidate(t, 1, peeled)
                if norms(peeled):
                    u = t.at(-1)
                    dve.wait_ge(rstd2_set, u.n + 1)
                    if peeled is None or peeled >= 2:
                        dve.wait_ge(result_set, u.n)
                    dve.scalar_tensor_tensor(out=shift[:], in0=norm[:, 1, :, 0], scalar=-1.0, in1=rstd[:, 1],
                                             op0=ALU.mult, op1=ALU.mult).then_inc(shift_set, 1)
                if turns_next(peeled):
                    low(t.at(1), at_hi, at_lo, at_hi_set, at_lo_set)
                if gates(peeled):
                    update(t, 1, peeled)

            steps(dve, step)


_INS = ["x", "src", "dst", "L0_gnn_W1", "L0_gnn_b1", "L0_gnn_W2", "L0_gnn_b2", "L0_gnn_w_ih", "L0_gnn_w_hh",
        "L0_gnn_b_ih", "L0_gnn_b_hh", "L0_gnn_gamma", "L0_gnn_beta"]


def kernel(**inputs):
    import numpy as _np
    import concourse.bacc as _bacc
    from concourse import mybir as _mybir
    from concourse.bass_utils import run_bass_kernel_spmd as _run

    nc = _bacc.Bacc("TRN2", target_bir_lowering=False, num_devices=1)
    arrays, args = {}, []
    for name in _INS:
        a = _np.ascontiguousarray(inputs[name])
        arrays[f"in_{name}_dram"] = a
        args.append(nc.dram_tensor(f"in_{name}_dram", a.shape, _mybir.dt.from_np(a.dtype), kind="ExternalInput").ap())
    shape = inputs["x"].shape
    args.append(nc.dram_tensor("out_0_dram", shape, _mybir.dt.float32, kind="ExternalOutput").ap())
    gnn_layer(nc, *args)
    r = _run(nc, [arrays], core_ids=[0])
    return r.results[0]["out_0_dram"]
```

```python
from contextlib import ExitStack

import concourse.bass as bass
from concourse import mybir

F32 = mybir.dt.float32
F32R = mybir.dt.float32r
BF16 = mybir.dt.bfloat16
I32 = mybir.dt.int32
ALU = mybir.AluOpType
ACT = mybir.ActivationFunctionType

P = 128
D = 256
KD = D // P
GATES = 3 * KD
EPS_COUNT = 1e-8
EPS_NORM = 1e-5

TILES = 2
PAIR = TILES * P
SUM = D + 1
AGG = D + 8
BLOCK = 512
ROWS = BLOCK // P

HH, IH, W1C = 0, KD * GATES * P, 2 * KD * GATES * P
W_COLS = W1C + 2 * KD * KD * P
BANK = 512
UNROLL = 4


class Gate:

    def __init__(self, engine, passed):
        self.engine, self.passed = engine, passed

    def take_waits(self):
        self.engine.sem_inc(self.passed, 1)


class Turn:

    def __init__(self, i, c, unroll=2):
        self.i, self.c, self.unroll = i, c, unroll

    def at(self, d):
        return Turn(self.i, self.c + d, self.unroll)

    @property
    def n(self):
        return self.unroll * self.i + self.c

    def below(self, n):
        return isinstance(self.n, int) and self.n < n

    @property
    def slot(self):
        return self.c % 2

    @property
    def slot4(self):
        return self.c % 4

    @property
    def use(self):
        return self.i + self.c // self.unroll


def turns(engine, step, first, last, end, unroll=2):
    for c in range(first):
        step(Turn(0, c, unroll), peeled=c)
    rounds = (last + 1 - first) // unroll
    with engine.Fori(0, rounds) as i:
        for c in range(unroll):
            step(Turn(i, first + c, unroll), peeled=None)
    for c in range(first + unroll * rounds, end):
        step(Turn(0, c, unroll), peeled=c)


def gnn_layer(nc, x, src, dst, w1, b1, w2, b2, w_ih, w_hh, b_ih, b_hh, gamma, beta, out):
    N, E = x.shape[0], src.shape[0]
    per_partition = -(-E // P)
    per_partition += per_partition % TILES
    pairs = per_partition // TILES
    full = E // per_partition
    rest = E - full * per_partition
    blocks = -(-N // BLOCK)
    last_parts = (N - (blocks - 1) * BLOCK) // ROWS
    spare = N
    agg_rows = N + P

    agg = nc.dram_tensor("agg", (agg_rows, AGG), F32).ap()

    with ExitStack() as whole:
        def keep(name, shape, dt):
            return whole.enter_context(nc.sbuf_tensor(name, shape, dt))

        ident = keep("ident", [P, P], F32)
        w_hi = keep("w_hi", [P, W_COLS], F32R)
        w_lo = keep("w_lo", [P, W_COLS], F32R)
        gate_bias = keep("gate_bias", [P, 2, GATES], F32)
        rz_bias = keep("rz_bias", [P, 2 * KD], F32)
        gamma_b = keep("gamma_b", [P, D], F32)
        beta_b = keep("beta_b", [P, D], F32)
        ps_a = whole.enter_context(nc.psum_tensor("ps_a", [P, 2, BANK], F32))
        ps_b = whole.enter_context(nc.psum_tensor("ps_b", [P, 2, BANK], F32))
        ps_c = whole.enter_context(nc.psum_tensor("ps_c", [P, BANK], F32))
        ps_d = whole.enter_context(nc.psum_tensor("ps_d", [P, BANK], F32))
        ps_e = whole.enter_context(nc.psum_tensor("ps_e", [P, 2, BANK], F32))

        edge_part(nc, x, src, dst, w1, b1, w2, b2, w_ih, w_hh, b_ih, b_hh, gamma, beta, agg,
                  per_partition, pairs, full, rest, spare,
                  ident, w_hi, w_lo, gate_bias, rz_bias, gamma_b, beta_b,
                  ps_a, ps_b, ps_c, ps_d, ps_e)
        node_part(nc, x, agg, out, blocks, last_parts,
                  ident, w_hi, w_lo, gate_bias, rz_bias, gamma_b, beta_b,
                  ps_a, ps_b, ps_c, ps_d, ps_e)


def edge_part(nc, x, src, dst, w1, b1, w2, b2, w_ih, w_hh, b_ih, b_hh, gamma, beta, agg,
              per_partition, pairs, full, rest, spare,
              ident, w_hi, w_lo, gate_bias, rz_bias, gamma_b, beta_b,
              ps_a, ps_b, ps_c, ps_d, ps_e):
    N = x.shape[0]
    with ExitStack() as ctx:
        def sb(name, shape, dt):
            return ctx.enter_context(nc.sbuf_tensor(name, shape, dt))

        def sem(name):
            return ctx.enter_context(nc.semaphore(name))

        agg_cols = agg.shape[0] * AGG // P
        agg_by_p = agg.rearrange("r d -> (r d)").rearrange("(p c) -> p c", p=P)
        clears = AGG // 8
        clear_cols = agg_cols // clears
        assert clear_cols * clears == agg_cols
        zeros = sb("zeros", [P, clear_cols], F32)

        w_hh_n = sb("w_hh_n", [P, GATES, D], F32)
        w_ih_n = sb("w_ih_n", [P, GATES, D], F32)
        w1_n = sb("w1_n", [P, KD, 2 * D], F32)
        w2_n = sb("w2_n", [P, KD, D], F32)
        w2_t = sb("w2_t", [P, KD, D], F32)
        b1_c = sb("b1_c", [P, KD], F32)
        b2_b = sb("b2_b", [P, D], F32)

        src_raw = sb("src_raw", [P, per_partition], I32)
        dst_raw = sb("dst_raw", [P, per_partition], I32)
        rows_f = sb("rows_f", [P, per_partition], F32)
        gather_idx = sb("gather_idx", [P, pairs, 2 * TILES], I32)
        scatter_idx = sb("scatter_idx", [P, pairs * TILES], I32)
        spare_f = sb("spare_f", [P, 1], F32)
        to_spare = sb("to_spare", [P, per_partition], F32)
        repeats = sb("repeats", [P, per_partition], F32)
        ones = sb("ones", [P, 1], BF16)
        earlier = sb("earlier", [P, 4, P], BF16)
        four_rows = sb("four_rows", [P, 2, 4], F32)
        same_all = sb("same_all", [P, per_partition, P], BF16)
        same_earlier = sb("same_earlier", [P, 2, 4, P], BF16)

        gidx = sb("gidx", [P, 4, 2 * TILES], I32)
        sidx = sb("sidx", [P, 4, TILES], I32)
        xe = sb("xe", [P, 4, 2 * TILES, D], F32)
        xt_hi = sb("xt_hi", [P, 2, 2 * KD, PAIR], F32R)
        xt_lo = sb("xt_lo", [P, 2, 2 * KD, PAIR], F32R)
        sig = sb("sig", [P, 2, KD, PAIR], F32)
        hid = sb("hid", [P, 2, KD, PAIR], F32)
        msg = sb("msg", [P, 2, TILES, SUM], F32)
        same = sb("same", [P, 2, TILES, P], F32)
        total = sb("total", [P, 4, TILES, SUM], F32)

        xt_ps = [ps_a, ps_b]
        hid_ps, msg_ps, total_ps = ps_c, ps_d, ps_e
        w_ps = [ps_a[:, 0], ps_a[:, 1], ps_b[:, 0], ps_b[:, 1]]
        rows_ps = [ps_c, ps_d]
        repeats_ps = ps_e[:, 0]

        pool_passed = sem("pool_passed")
        zeroed_tile = sem("zeroed_tile")
        cleared = sem("cleared")
        weights_in = sem("weights_in")
        bias_in = sem("bias_in")
        edges_in = sem("edges_in")
        pads_set = sem("pads_set")
        ident_zero = sem("ident_zero")
        consts_set = sem("consts_set")
        keys = sem("keys")
        w_turned = sem("w_turned")
        w_hi_done = sem("w_hi_done")
        w_lo_done = sem("w_lo_done")
        four_copied = sem("four_copied")
        rows_spread = sem("rows_spread")
        same_set = sem("same_set")
        masked = sem("masked")
        repeats_counted = sem("repeats_counted")
        scatter_step = sem("scatter_step")
        scatter_set = sem("scatter_set")
        gidx_set = sem("gidx_set")
        gathered = [sem(f"gathered{s}") for s in range(4)]
        xt_turned = sem("xt_turned")
        xt_hi_set = sem("xt_hi_set")
        xt_lo_set = sem("xt_lo_set")
        hid_summed = sem("hid_summed")
        sig_set = sem("sig_set")
        hid_set = sem("hid_set")
        msg_summed = sem("msg_summed")
        msg_set = sem("msg_set")
        same_f_set = sem("same_f_set")
        total_summed = sem("total_summed")
        total_set = sem("total_set")
        added = sem("added")

        chunks = [(w_hh_n, k, m) for k in range(KD) for m in range(GATES)]
        chunks += [(w_ih_n, k, m) for k in range(KD) for m in range(GATES)]
        chunks += [(w1_n, k, m) for k in range(2 * KD) for m in range(KD)]
        chunks += [(w2_n, k, m) for k in range(KD) for m in range(KD)]
        groups = [chunks[g:g + 4] for g in range(0, len(chunks), 4)]
        split_groups = W_COLS // BANK
        quads = per_partition // 4
        assert per_partition % 4 == 0 and pairs % 2 == 0 and len(groups) == split_groups + 1

        block = ctx.enter_context(nc.Block())

        @block.sync
        def _(sp):
            sp.wait_ge(pads_set, 2)
            for raw, edge in ((src_raw, src), (dst_raw, dst)):
                sp.dma_start(raw[0:full, :], edge[0:full * per_partition].rearrange(
                    "(p c) -> p c", p=full)).then_inc(edges_in, 16)
                if rest:
                    sp.dma_start(raw[full:full + 1, 0:rest], edge[full * per_partition:].rearrange(
                        "(p c) -> p c", p=1)).then_inc(edges_in, 16)
            for nat, w in ((w_hh_n, w_hh), (w_ih_n, w_ih), (w1_n, w1), (w2_n, w2)):
                sp.dma_start(nat[:], w.rearrange("(m p) k -> p m k", p=P)).then_inc(weights_in, 16)
            with nc.allow_non_contiguous_dma(reason="a few bias columns"):
                sp.dma_start(b1_c[:], b1.rearrange("(c p) -> p c", p=P)).then_inc(bias_in, 16)
                sp.dma_start(gate_bias[:, 0], b_ih.rearrange("(c p) -> p c", p=P)).then_inc(bias_in, 16)
                sp.dma_start(gate_bias[:, 1], b_hh.rearrange("(c p) -> p c", p=P)).then_inc(bias_in, 16)
            for row, v in ((b2_b, b2), (gamma_b, gamma), (beta_b, beta)):
                sp.dma_start(row[:], v.rearrange("(a d) -> a d", a=1).to_broadcast([P, D])).then_inc(bias_in, 16)
            sp.wait_ge(zeroed_tile, 1)
            with sp.Fori(0, clears) as c:
                sp.dma_start(agg_by_p[:, bass.ds(c * clear_cols, clear_cols)], zeros[:]).then_inc(cleared, 16)

        @block.gpsimd
        def _(pool):
            pool.memset(src_raw[:], spare + P - 1).then_inc(pads_set, 1)
            pool.memset(dst_raw[:], 0).then_inc(pads_set, 1)
            pool.memset(ident[:], 0.0).then_inc(ident_zero, 1)
            pool.memset(earlier[:], 1.0).then_inc(ident_zero, 1)
            pool.memset(ones[:], 1.0).then_inc(consts_set, 1)
            pool.wait_ge(ident_zero, 2)
            pool.affine_select(out=ident[:], in_=ident[:], compare_op=ALU.not_equal, fill=1.0, base=0,
                               pattern=[[-1, P]], channel_multiplier=1).then_inc(consts_set, 1)
            pool.affine_select(out=earlier[:], in_=earlier[:], compare_op=ALU.is_gt, fill=0.0, base=0,
                               pattern=[[0, 4], [1, P]], channel_multiplier=-1).then_inc(consts_set, 1)
            pool.iota(spare_f[:], [[0, 1]], base=spare, channel_multiplier=1,
                      allow_small_or_imprecise_dtypes=True).then_inc(consts_set, 1)
            pool.memset(msg[:, :, :, D:SUM], 1.0).then_inc(consts_set, 1)

            gate = Gate(pool, pool_passed)

            def gather(t, tile):
                if tile == 0:
                    pool.wait_ge(gidx_set, t.n + 1)
                    if not t.below(4):
                        pool.wait_ge(xt_turned, t.n - 3)
                    gate.take_waits()
                for j in (2 * tile, 2 * tile + 1):
                    pool.indirect_dma_start(
                        out=xe[:, t.slot4, j, :], out_offset=None, in_=x[:, :],
                        in_offset=bass.IndirectOffsetOnAxis(ap=gidx[:, t.slot4, j:j + 1], axis=0),
                    ).then_inc(gathered[t.slot4], 16)

            def add(t, tile):
                if tile == 0:
                    pool.wait_ge(total_set, 2 * (t.n + 1))
                if not (tile == 0 and t.below(1)):
                    pool.wait_ge(added, 16 * (TILES * t.n + tile))
                gate.take_waits()
                pool.indirect_dma_start(
                    out=agg[:, :], in_=total[:, t.slot4, tile, :], in_offset=None,
                    out_offset=bass.IndirectOffsetOnAxis(ap=sidx[:, t.slot4, tile:tile + 1], axis=0),
                    compute_op=ALU.add,
                ).then_inc(added, 16)

            LAG = 6

            def step(t, peeled):
                if peeled == LAG:
                    pool.wait_ge(cleared, 16 * clears)
                for tile in range(TILES):
                    if peeled is None or peeled >= LAG:
                        add(t.at(-LAG), tile)
                    if peeled is None or peeled < pairs:
                        gather(t, tile)

            turns(pool, step, LAG + 1, pairs - 1, pairs + LAG, UNROLL)
            pool.wait_ge(added, 16 * TILES * pairs)

        @block.scalar
        def _(act):
            for g, group in enumerate(groups):
                act.wait_ge(w_turned, g + 1)
                if g < split_groups:
                    act.copy(w_hi[:, g * BANK:(g + 1) * BANK], w_ps[g % 4]).then_inc(w_hi_done, 1)
                else:
                    act.copy(w2_t[:].rearrange("p k d -> p (k d)"), w_ps[g % 4]).then_inc(w_hi_done, 1)
            act.wait_ge(bias_in, 96)

            def split_x(t):
                act.wait_ge(xt_turned, t.n + 1)
                if not t.below(2):
                    act.wait_ge(hid_summed, t.n - 1)
                act.copy(xt_hi[:, t.slot].rearrange("p k e -> p (k e)"),
                         xt_ps[t.slot][:].rearrange("p k e -> p (k e)")).then_inc(xt_hi_set, 1)

            def step(t, peeled):
                first = peeled == 0
                if first:
                    split_x(t)
                if peeled is None or peeled < pairs:
                    act.wait_ge(hid_summed, t.n + 1)
                    if peeled is None or peeled >= 2:
                        act.wait_ge(hid_set, t.n - 1)
                    for m in range(KD):
                        ins = act.activation(sig[:, t.slot, m], hid_ps[:, m * PAIR:(m + 1) * PAIR],
                                             ACT.Sigmoid, bias=b1_c[:, m:m + 1])
                    ins.then_inc(sig_set, 1)
                if peeled is None or peeled + 1 < pairs:
                    split_x(t.at(1))
                if peeled is None or peeled < pairs:
                    if peeled == 0:
                        act.wait_ge(scatter_set, 1)
                    if peeled is None or peeled >= 2:
                        act.wait_ge(total_summed, t.n - 1)
                    act.copy(same[:, t.slot].rearrange("p t e -> p (t e)"),
                             same_all[:, bass.ds(t.n * TILES, TILES), :].rearrange("p t e -> p (t e)")
                             ).then_inc(same_f_set, 1)
                if peeled is None or peeled >= 2:
                    u = t.at(-2)
                    act.wait_ge(total_summed, u.n + 1)
                    if peeled is None or peeled >= 6:
                        act.wait_ge(added, 16 * TILES * (u.n - 3))
                    act.copy(sidx[:, u.slot4], scatter_idx[:, bass.ds(u.n * TILES, TILES)]).then_inc(total_set, 1)
                    act.copy(total[:, u.slot4], total_ps[:, :, 0:SUM]).then_inc(total_set, 1)

            turns(act, step, 6, pairs - 5, pairs + 2, UNROLL)

        @block.tensor
        def _(pe):
            pe.wait_ge(consts_set, 5)
            pe.wait_ge(weights_in, 64)
            for g, group in enumerate(groups):
                if g >= 4:
                    pe.wait_ge(w_hi_done, g - 3)
                    pe.wait_ge(w_lo_done, g - 3)
                for c, (nat, k, m) in enumerate(group):
                    ins = pe.transpose(w_ps[g % 4][:, c * P:(c + 1) * P], nat[:, m, k * P:(k + 1) * P], ident[:])
                ins.then_inc(w_turned, 1)

            def spread(t):
                pe.wait_ge(four_copied, t.n + 1)
                if not t.below(2):
                    pe.wait_ge(same_set, t.n - 1)
                for j in range(4):
                    ins = pe.transpose(rows_ps[t.slot][:, j * P:(j + 1) * P],
                                       four_rows[:, t.slot, j:j + 1].to_broadcast([P, P]), ident[:])
                ins.then_inc(rows_spread, 1)

            def count_repeats(t):
                pe.wait_ge(masked, t.n + 1)
                for j in range(4):
                    ins = pe.matmul(repeats_ps[:, bass.ds(t.n * 4 + j, 1)], same_earlier[:, t.slot, j],
                                    ones[:], start=True, stop=True)
                ins.then_inc(repeats_counted, 1)

            def leader_step(t, peeled):
                if peeled is None or peeled < quads:
                    spread(t)
                if peeled is None or peeled >= 1:
                    count_repeats(t.at(-1))

            turns(pe, leader_step, 3, quads - 2, quads + 1)

            def turn_x(t):
                pe.wait_ge(gathered[t.slot4], 64 * (t.use + 1))
                if not t.below(2):
                    pe.wait_ge(xt_hi_set, t.n - 1)
                    pe.wait_ge(xt_lo_set, t.n - 1)
                for e in range(TILES):
                    for k in range(2 * KD):
                        ins = pe.transpose(
                            xt_ps[t.slot][:].rearrange("p a (b e) -> p (a b) e", b=2)[:, k, e * P:(e + 1) * P],
                            xe[:, t.slot4, 2 * e + k // KD, (k % KD) * P:(k % KD + 1) * P], ident[:])
                ins.then_inc(xt_turned, 1)

            def hidden(t, peeled):
                pe.wait_ge(xt_hi_set, t.n + 1)
                pe.wait_ge(xt_lo_set, t.n + 1)
                if peeled is None or peeled >= 1:
                    pe.wait_ge(hid_set, t.n)
                for m in range(KD):
                    acc = hid_ps[:, m * PAIR:(m + 1) * PAIR]
                    for k in range(2 * KD):
                        cols = slice(W1C + (k * KD + m) * P, W1C + (k * KD + m + 1) * P)
                        pe.matmul(acc, w_hi[:, cols], xt_hi[:, t.slot, k], start=(k == 0), stop=False)
                        pe.matmul(acc, w_hi[:, cols], xt_lo[:, t.slot, k], start=False, stop=False)
                        ins = pe.matmul(acc, w_lo[:, cols], xt_hi[:, t.slot, k], start=False,
                                        stop=(k == 2 * KD - 1))
                ins.then_inc(hid_summed, 1)

            def message(t, peeled):
                pe.wait_ge(hid_set, t.n + 1)
                if peeled is None or peeled >= 2:
                    pe.wait_ge(msg_set, t.n)
                for j in range(TILES):
                    for k in range(KD):
                        ins = pe.matmul(msg_ps[:, j * D:(j + 1) * D], hid[:, t.slot, k, j * P:(j + 1) * P],
                                        w2_t[:, k], start=(k == 0), stop=(k == KD - 1))
                ins.then_inc(msg_summed, 1)

            def sums(t, peeled):
                pe.wait_ge(msg_set, t.n + 1)
                pe.wait_ge(same_f_set, t.n + 1)
                if peeled is None or peeled >= 3:
                    pe.wait_ge(total_set, 2 * t.n)
                for j in range(TILES):
                    ins = pe.matmul(total_ps[:, j, 0:SUM], same[:, t.slot, j], msg[:, t.slot, j],
                                    start=True, stop=True)
                ins.then_inc(total_summed, 1)

            def step(t, peeled):
                if peeled == 0:
                    pe.wait_ge(w_hi_done, len(groups))
                    pe.wait_ge(w_lo_done, split_groups)
                    turn_x(t)
                if peeled is None or peeled < pairs:
                    hidden(t, peeled)
                if peeled is None or peeled + 1 < pairs:
                    turn_x(t.at(1))
                if peeled is None or 1 <= peeled <= pairs:
                    message(t.at(-1), peeled)
                if peeled is None or peeled >= 2:
                    sums(t.at(-2), peeled)

            turns(pe, step, 6, pairs - 5, pairs + 2, UNROLL)

        @block.vector
        def _(dve):
            dve.memset(zeros[:], 0.0).then_inc(zeroed_tile, 1)

            dve.wait_ge(edges_in, 64 if rest else 32)
            g4 = gather_idx[:].rearrange("p q (t s) -> p q t s", s=2)
            as_pairs = lambda a: a.rearrange("p (q t) -> p q t", t=TILES)
            dve.tensor_scalar(g4[:, :, :, 0], as_pairs(src_raw[:]), float(N - 1), None, ALU.min).then_inc(keys, 1)
            dve.tensor_copy(g4[:, :, :, 1], as_pairs(dst_raw[:])).then_inc(keys, 1)
            dve.wait_ge(keys, 2)

            def copy_gidx(t):
                dve.tensor_copy(gidx[:, t.slot4], gather_idx[:, bass.ds(t.n, 1), :].rearrange(
                    "p q j -> p (q j)")).then_inc(gidx_set, 1)

            for c in range(4):
                copy_gidx(Turn(0, c, UNROLL))
            dve.tensor_copy(rows_f[:], src_raw[:]).then_inc(keys, 1)
            dve.wait_ge(keys, 3)

            for g in range(split_groups):
                dve.wait_ge(w_hi_done, g + 1)
                cols = slice(g * BANK, (g + 1) * BANK)
                dve.tensor_tensor(w_lo[:, cols], w_ps[g % 4], w_hi[:, cols].bitcast(F32),
                                  ALU.subtract).then_inc(w_lo_done, 1)
            dve.wait_ge(consts_set, 5)

            def copy_rows(t):
                if not t.below(2):
                    dve.wait_ge(rows_spread, t.n - 1)
                dve.tensor_copy(four_rows[:, t.slot], rows_f[:, bass.ds(t.n * 4, 4)]).then_inc(four_copied, 1)

            def compare(t):
                dve.wait_ge(rows_spread, t.n + 1)
                four = same_all[:, bass.ds(t.n * 4, 4), :]
                dve.tensor_tensor(four, rows_ps[t.slot][:].rearrange("p (t e) -> p t e", t=4),
                                  rows_f[:, bass.ds(t.n * 4, 4)].unsqueeze(2).to_broadcast([P, 4, P]),
                                  ALU.is_equal).then_inc(same_set, 1)
                dve.wait_ge(same_set, t.n + 1)
                if not t.below(2):
                    dve.wait_ge(repeats_counted, t.n - 1)
                dve.tensor_tensor(same_earlier[:, t.slot], four, earlier[:], ALU.mult).then_inc(masked, 1)

            def leader_step(t, peeled):
                if peeled is None or peeled < quads:
                    copy_rows(t)
                if peeled is None or peeled >= 1:
                    compare(t.at(-1))

            turns(dve, leader_step, 3, quads - 2, quads + 1)

            dve.wait_ge(repeats_counted, quads)
            dve.tensor_scalar(repeats[:], repeats_ps[:, 0:per_partition], 1.0, None, ALU.min).then_inc(scatter_step, 1)
            dve.tensor_scalar(to_spare[:], rows_f[:], -1.0, spare_f[:, 0:1], ALU.mult, ALU.add).then_inc(scatter_step, 1)
            dve.wait_ge(scatter_step, 2)
            dve.tensor_tensor(repeats[:], repeats[:], to_spare[:], ALU.mult).then_inc(scatter_step, 1)
            dve.wait_ge(scatter_step, 3)
            dve.tensor_tensor(scatter_idx[:], repeats[:], rows_f[:], ALU.add).then_inc(scatter_set, 1)
            dve.wait_ge(bias_in, 96)
            dve.tensor_tensor(rz_bias[:], gate_bias[:, 0, 0:2 * KD], gate_bias[:, 1, 0:2 * KD],
                              ALU.add).then_inc(scatter_step, 1)

            def low_x(t):
                dve.wait_ge(xt_hi_set, t.n + 1)
                if not t.below(2):
                    dve.wait_ge(hid_summed, t.n - 1)
                dve.tensor_tensor(xt_lo[:, t.slot].rearrange("p k e -> p (k e)"),
                                  xt_ps[t.slot][:].rearrange("p k e -> p (k e)"),
                                  xt_hi[:, t.slot].rearrange("p k e -> p (k e)").bitcast(F32),
                                  ALU.subtract).then_inc(xt_lo_set, 1)

            def step(t, peeled):
                if peeled == 0:
                    low_x(t)
                if peeled is None or peeled < pairs:
                    dve.wait_ge(sig_set, t.n + 1)
                    if peeled is None or peeled >= 2:
                        dve.wait_ge(msg_summed, t.n - 1)
                    for m in range(KD):
                        ins = dve.scalar_tensor_tensor(
                            out=hid[:, t.slot, m], in0=hid_ps[:, m * PAIR:(m + 1) * PAIR], scalar=b1_c[:, m:m + 1],
                            in1=sig[:, t.slot, m], op0=ALU.add, op1=ALU.mult)
                    ins.then_inc(hid_set, 1)
                if peeled is None or peeled + 1 < pairs:
                    low_x(t.at(1))
                if peeled is None or peeled + 4 < pairs:
                    dve.wait_ge(xt_turned, t.n + 1)
                    copy_gidx(t.at(4))
                if peeled is None or 1 <= peeled <= pairs:
                    u = t.at(-1)
                    dve.wait_ge(msg_summed, u.n + 1)
                    if peeled is None or peeled >= 3:
                        dve.wait_ge(total_summed, u.n - 1)
                    dve.tensor_tensor(msg[:, u.slot, :, 0:D], msg_ps[:].rearrange("p (t d) -> p t d", t=TILES),
                                      b2_b[:].unsqueeze(1).to_broadcast([P, TILES, D]), ALU.add).then_inc(msg_set, 1)

            turns(dve, step, 6, pairs - 5, pairs + 2, UNROLL)


def node_part(nc, x, agg, out, blocks, last_parts,
              ident, w_hi, w_lo, gate_bias, rz_bias, gamma_b, beta_b,
              ps_a, ps_b, ps_c, ps_d, ps_e):
    with ExitStack() as ctx:
        def sb(name, shape, dt):
            return ctx.enter_context(nc.sbuf_tensor(name, shape, dt))

        def sem(name):
            return ctx.enter_context(nc.semaphore(name))

        x_in = sb("x_in", [P, 2, ROWS, D], F32)
        a_in = sb("a_in", [P, 2, ROWS, AGG], F32)
        count_eps = sb("count_eps", [P, 2, ROWS], F32)
        inv_count = sb("inv_count", [P, 2, ROWS], F32)
        mean = sb("mean", [P, 2, ROWS, D], F32)
        x_beta = sb("x_beta", [P, 2, ROWS, D], F32)
        unit = sb("unit", [P, ROWS, D], F32)
        scaled = sb("scaled", [P, ROWS, D], F32)
        resid = sb("resid", [P, 2, ROWS, D], F32)
        result = sb("result", [P, 2, ROWS, D], F32)
        xt = sb("xt", [P, 2, KD, BLOCK], F32)
        xt_hi = sb("nxt_hi", [P, 2, KD, BLOCK], F32R)
        xt_lo = sb("nxt_lo", [P, 2, KD, BLOCK], F32R)
        at_hi = sb("at_hi", [P, 2, KD, BLOCK], F32R)
        at_lo = sb("at_lo", [P, 2, KD, BLOCK], F32R)
        r = sb("r", [P, KD, BLOCK], F32)
        z = sb("z", [P, KD, BLOCK], F32)
        pre = sb("pre", [P, KD, BLOCK], F32)
        cand = sb("cand", [P, KD, BLOCK], F32)
        diff = sb("diff", [P, KD, BLOCK], F32)
        new = sb("new", [P, KD, BLOCK], F32)
        stats = sb("stats", [P, 2, ROWS, 6], F32)
        norm = sb("norm", [P, 2, ROWS, 2], F32)
        var_eps = sb("var_eps", [P, 2, ROWS], F32)
        rstd = sb("rstd", [P, 2, ROWS], F32)
        shift = sb("shift", [P, 2, ROWS], F32)
        minus_half = sb("minus_half", [P, ROWS], F32)

        turn_ps = ps_a
        back = ps_b[:].rearrange("p a (b d) -> p (a b) d", d=D)
        r_ps, z_ps, h_ps, i_ps = ps_c, ps_d, ps_e[:, 0], ps_e[:, 1]

        x_landed = [sem("x_landed0"), sem("x_landed1")]
        a_landed = [sem("a_landed0"), sem("a_landed1")]
        stored = [sem("stored0"), sem("stored1")]
        dve_passed = sem("dve_passed")
        half_set = sem("half_set")
        count_eps_set = sem("count_eps_set")
        inv_count_set = sem("inv_count_set")
        mean_set = sem("mean_set")
        x_beta_set = sem("x_beta_set")
        x_turned = sem("x_turned")
        a_turned = sem("a_turned")
        xt_set = sem("xt_set")
        xt_hi_set = sem("nxt_hi_set")
        xt_lo_set = sem("nxt_lo_set")
        at_hi_set = sem("at_hi_set")
        at_lo_set = sem("at_lo_set")
        r_summed = sem("r_summed")
        z_summed = sem("z_summed")
        h_summed = sem("h_summed")
        i_summed = sem("i_summed")
        r_set = sem("r_set")
        z_set = sem("z_set")
        rh_set = sem("rh_set")
        pre_set = sem("pre_set")
        cand_set = sem("cand_set")
        diff_set = sem("diff_set")
        zdiff_set = sem("zdiff_set")
        new_set = sem("new_set")
        new_turned = sem("new_turned")
        stats1_set = sem("stats1_set")
        norm1_set = sem("norm1_set")
        var1_set = sem("var1_set")
        rstd1_set = sem("rstd1_set")
        shift1_set = sem("shift1_set")
        unit_set = sem("unit_set")
        scaled_set = sem("scaled_set")
        resid_set = sem("resid_set")
        stats2_set = sem("stats2_set")
        norm2_set = sem("norm2_set")
        var2_set = sem("var2_set")
        rstd2_set = sem("rstd2_set")
        shift2_set = sem("shift2_set")
        result_set = sem("result_set")

        def rows_of(a, n, parts=P):
            return a[bass.ds(n * BLOCK, parts * ROWS), :].rearrange("(p j) d -> p j d", j=ROWS)

        def steps(engine, step, first=3):
            turns(engine, step, first, blocks - 4, blocks + 1)

        def gates(peeled):
            return peeled is None or peeled < blocks

        def turns_next(peeled):
            return peeled is None or peeled + 1 < blocks

        def norms(peeled):
            return peeled is None or peeled >= 1

        block = ctx.enter_context(nc.Block())

        @block.sync
        def _(sp):
            def load(t, parts):
                if not t.below(2):
                    sp.wait_ge(x_turned, t.n - 1)
                    sp.wait_ge(x_beta_set, t.n - 1)
                sp.dma_start(x_in[0:parts, t.slot], rows_of(x, t.n, parts)).then_inc(x_landed[t.slot], 16)
                if not t.below(2):
                    sp.wait_ge(mean_set, t.n - 1)
                sp.dma_start(a_in[0:parts, t.slot], rows_of(agg, t.n, parts)).then_inc(a_landed[t.slot], 16)

            def store(t, parts):
                sp.wait_ge(result_set, t.n + 1)
                sp.dma_start(rows_of(out, t.n, parts), result[0:parts, t.slot]).then_inc(stored[t.slot], 16)

            def step(t, peeled):
                if peeled == 0:
                    load(t, P)
                    load(t.at(1), P)
                if peeled is None or peeled + 2 < blocks:
                    load(t.at(2), last_parts if peeled == blocks - 3 else P)
                if norms(peeled):
                    store(t.at(-1), last_parts if peeled == blocks else P)

            steps(sp, step)
            sp.wait_ge(stored[0], 16 * ((blocks + 1) // 2))
            sp.wait_ge(stored[1], 16 * (blocks // 2))

        @block.gpsimd
        def _(pool):
            pool.memset(minus_half[:], -0.5).then_inc(half_set, 1)
            pool.wait_ge(half_set, 1)

            def prepare(t):
                pool.wait_ge(inv_count_set, t.n + 1)
                if not t.below(2):
                    pool.wait_ge(a_turned, t.n - 1)
                pool.tensor_tensor(mean[:, t.slot], a_in[:, t.slot, :, 0:D],
                                   inv_count[:, t.slot].unsqueeze(2).to_broadcast([P, ROWS, D]),
                                   ALU.mult).then_inc(mean_set, 1)

            def add_beta(t):
                pool.wait_ge(x_landed[t.slot], 16 * (t.use + 1))
                if not t.below(2):
                    pool.wait_ge(resid_set, t.n - 1)
                pool.tensor_tensor(x_beta[:, t.slot], x_in[:, t.slot],
                                   beta_b[:].unsqueeze(1).to_broadcast([P, ROWS, D]), ALU.add).then_inc(x_beta_set, 1)

            def difference(t, h, peeled):
                pool.wait_ge(cand_set, 2 * t.n + h + 1)
                if peeled is None or peeled >= 1:
                    pool.wait_ge(zdiff_set, 2 * t.n + h - 1)
                pool.tensor_tensor(diff[:, h], xt[:, t.slot, h], cand[:, h], ALU.subtract).then_inc(diff_set, 1)

            def low_x(t):
                pool.wait_ge(xt_set, t.n + 1)
                if not t.below(2):
                    pool.wait_ge(z_summed, 2 * (t.n - 1))
                pool.tensor_tensor(xt_lo[:, t.slot].rearrange("p k n -> p (k n)"),
                                   xt[:, t.slot].rearrange("p k n -> p (k n)"),
                                   xt_hi[:, t.slot].rearrange("p k n -> p (k n)").bitcast(F32),
                                   ALU.subtract).then_inc(xt_lo_set, 1)

            def root(t, which, var_set, rstd_set):
                pool.wait_ge(var_set, t.n + 1)
                pool.tensor_tensor(rstd[:, which], var_eps[:, which], minus_half[:], ALU.pow).then_inc(rstd_set, 1)

            def step(t, peeled):
                if peeled == 0:
                    prepare(t)
                    low_x(t)
                if turns_next(peeled):
                    prepare(t.at(1))
                if gates(peeled):
                    add_beta(t)
                    difference(t, 0, peeled)
                if norms(peeled):
                    root(t.at(-1), 0, var1_set, rstd1_set)
                if turns_next(peeled):
                    low_x(t.at(1))
                if gates(peeled):
                    difference(t, 1, peeled)
                if norms(peeled):
                    root(t.at(-1), 1, var2_set, rstd2_set)

            steps(pool, step)

        @block.scalar
        def _(act):
            def high(t, turned, hi, hi_set):
                act.wait_ge(turned, t.n + 1)
                if not t.below(2):
                    act.wait_ge(z_summed, 2 * (t.n - 1))
                act.copy(hi[:, t.slot].rearrange("p k n -> p (k n)"),
                         turn_ps[:].rearrange("p k n -> p (k n)")).then_inc(hi_set, 1)

            def keep_x(t):
                if not t.below(2):
                    act.wait_ge(diff_set, 2 * (t.n - 1))
                act.copy(xt[:, t.slot].rearrange("p k n -> p (k n)"),
                         turn_ps[:].rearrange("p k n -> p (k n)")).then_inc(xt_set, 1)

            def reset(t, h, peeled):
                act.wait_ge(r_summed, 2 * t.n + h + 1)
                if peeled is None or peeled >= 1:
                    act.wait_ge(rh_set, 2 * t.n + h - 1)
                act.activation(r[:, h], r_ps[:], ACT.Sigmoid, bias=rz_bias[:, h:h + 1]).then_inc(r_set, 1)

            def keep_gate(t, h, peeled):
                act.wait_ge(z_summed, 2 * t.n + h + 1)
                if peeled is None or peeled >= 1:
                    act.wait_ge(zdiff_set, 2 * t.n + h - 1)
                act.activation(z[:, h], z_ps[:], ACT.Sigmoid, bias=rz_bias[:, KD + h:KD + h + 1]).then_inc(z_set, 1)

            def tanh(t, h, peeled):
                act.wait_ge(pre_set, 2 * t.n + h + 1)
                if peeled is None or peeled >= 1:
                    act.wait_ge(new_set, 2 * t.n + h - 1)
                act.activation(cand[:, h], pre[:, h], ACT.Tanh,
                               bias=gate_bias[:, 0, 2 * KD + h:2 * KD + h + 1]).then_inc(cand_set, 1)

            def normalise_state(t, peeled):
                act.wait_ge(shift1_set, t.n + 1)
                if peeled is None or peeled >= 2:
                    act.wait_ge(scaled_set, t.n)
                for j in range(ROWS):
                    ins = act.activation(unit[:, j], back[:, j], ACT.Identity,
                                         bias=shift[:, 0, j:j + 1], scale=rstd[:, 0, j:j + 1])
                ins.then_inc(unit_set, 1)

            def normalise_result(t):
                act.wait_ge(shift2_set, t.n + 1)
                if not t.below(2):
                    act.wait_ge(stored[t.slot], 16 * t.use)
                for j in range(ROWS):
                    ins = act.activation(result[:, t.slot, j], resid[:, t.slot, j], ACT.Identity,
                                         bias=shift[:, 1, j:j + 1], scale=rstd[:, 1, j:j + 1])
                ins.then_inc(result_set, 1)

            def step(t, peeled):
                if peeled == 0:
                    high(t, x_turned, xt_hi, xt_hi_set)
                    keep_x(t)
                    high(t, a_turned, at_hi, at_hi_set)
                if gates(peeled):
                    reset(t, 0, peeled)
                if peeled is None or peeled >= 2:
                    normalise_result(t.at(-2))
                if turns_next(peeled):
                    high(t.at(1), x_turned, xt_hi, xt_hi_set)
                if gates(peeled):
                    tanh(t, 0, peeled)
                if turns_next(peeled):
                    keep_x(t.at(1))
                if gates(peeled):
                    keep_gate(t, 0, peeled)
                if norms(peeled):
                    normalise_state(t.at(-1), peeled)
                if gates(peeled):
                    reset(t, 1, peeled)
                if turns_next(peeled):
                    high(t.at(1), a_turned, at_hi, at_hi_set)
                if gates(peeled):
                    tanh(t, 1, peeled)
                    keep_gate(t, 1, peeled)

            steps(act, step, 4)
            normalise_result(Turn(0, blocks - 1))

        @block.tensor
        def _(pe):
            def turn(rows, t, done):
                for j in range(ROWS):
                    for k in range(KD):
                        ins = pe.transpose(turn_ps[:, k, j * P:(j + 1) * P], rows[:, t.slot, j, k * P:(k + 1) * P],
                                           ident[:])
                ins.then_inc(done, 1)

            def turn_x(t):
                pe.wait_ge(x_landed[t.slot], 16 * (t.use + 1))
                if not t.below(1):
                    pe.wait_ge(at_lo_set, t.n)
                turn(x_in, t, x_turned)

            def turn_mean(t):
                pe.wait_ge(mean_set, t.n + 1)
                pe.wait_ge(xt_set, t.n + 1)
                turn(mean, t, a_turned)

            def products(acc, base, chunk, hi, lo, slot, start, stop):
                for k in range(KD):
                    cols = slice(base + (k * GATES + chunk) * P, base + (k * GATES + chunk + 1) * P)
                    pe.matmul(acc, w_hi[:, cols], hi[:, slot, k], start=(start and k == 0), stop=False)
                    pe.matmul(acc, w_hi[:, cols], lo[:, slot, k], start=False, stop=False)
                    ins = pe.matmul(acc, w_lo[:, cols], hi[:, slot, k], start=False, stop=(stop and k == KD - 1))
                return ins

            def sum_h(t, h, peeled):
                if h == 0:
                    pe.wait_ge(xt_hi_set, t.n + 1)
                    pe.wait_ge(xt_lo_set, t.n + 1)
                if peeled is None or peeled >= 1 or h == 1:
                    pe.wait_ge(rh_set, 2 * t.n + h)
                products(h_ps, HH, 2 * KD + h, xt_hi, xt_lo, t.slot, True, True).then_inc(h_summed, 1)

            def sum_r(t, h, peeled):
                if peeled is None or peeled >= 1 or h == 1:
                    pe.wait_ge(r_set, 2 * t.n + h)
                products(r_ps[:], HH, h, xt_hi, xt_lo, t.slot, True, False)
                if h == 0:
                    pe.wait_ge(at_hi_set, t.n + 1)
                    pe.wait_ge(at_lo_set, t.n + 1)
                products(r_ps[:], IH, h, at_hi, at_lo, t.slot, False, True).then_inc(r_summed, 1)

            def sum_i(t, h, peeled):
                if peeled is None or peeled >= 1 or h == 1:
                    pe.wait_ge(pre_set, 2 * t.n + h)
                products(i_ps, IH, 2 * KD + h, at_hi, at_lo, t.slot, True, True).then_inc(i_summed, 1)

            def sum_z(t, h, peeled):
                if peeled is None or peeled >= 1 or h == 1:
                    pe.wait_ge(z_set, 2 * t.n + h)
                products(z_ps[:], HH, KD + h, xt_hi, xt_lo, t.slot, True, False)
                products(z_ps[:], IH, KD + h, at_hi, at_lo, t.slot, False, True).then_inc(z_summed, 1)

            def turn_back(t, h, peeled):
                pe.wait_ge(new_set, 2 * t.n + h + 1)
                if h == 0 and (peeled is None or peeled >= 1):
                    pe.wait_ge(unit_set, t.n)
                for j in range(ROWS):
                    ins = pe.transpose(back[:, j, h * P:(h + 1) * P], new[:, h, j * P:(j + 1) * P], ident[:])
                ins.then_inc(new_turned, 1)

            def step(t, peeled):
                if peeled == 0:
                    turn_x(t)
                    turn_mean(t)
                if gates(peeled):
                    sum_h(t, 0, peeled)
                    sum_r(t, 0, peeled)
                    sum_i(t, 0, peeled)
                if norms(peeled):
                    turn_back(t.at(-1), 1, peeled)
                if turns_next(peeled):
                    turn_x(t.at(1))
                if gates(peeled):
                    sum_z(t, 0, peeled)
                    sum_h(t, 1, peeled)
                    sum_r(t, 1, peeled)
                if turns_next(peeled):
                    turn_mean(t.at(1))
                if gates(peeled):
                    sum_i(t, 1, peeled)
                    turn_back(t, 0, peeled)
                    sum_z(t, 1, peeled)

            steps(pe, step)

        @block.vector
        def _(dve):
            gate = Gate(dve, dve_passed)

            def invert_count(t):
                dve.wait_ge(a_landed[t.slot], 16 * (t.use + 1))
                if not t.below(2):
                    dve.wait_ge(mean_set, t.n - 1)
                dve.tensor_scalar(count_eps[:, t.slot], a_in[:, t.slot, :, D], EPS_COUNT, None,
                                  ALU.add).then_inc(count_eps_set, 1)
                dve.wait_ge(count_eps_set, t.n + 1)
                gate.take_waits()
                dve.reciprocal(inv_count[:, t.slot], count_eps[:, t.slot]).then_inc(inv_count_set, 1)

            def low_mean(t):
                dve.wait_ge(at_hi_set, t.n + 1)
                if not t.below(2):
                    dve.wait_ge(z_summed, 2 * (t.n - 1))
                dve.tensor_tensor(at_lo[:, t.slot].rearrange("p k n -> p (k n)"),
                                  turn_ps[:].rearrange("p k n -> p (k n)"),
                                  at_hi[:, t.slot].rearrange("p k n -> p (k n)").bitcast(F32),
                                  ALU.subtract).then_inc(at_lo_set, 1)

            def reset_h(t, h, peeled):
                dve.wait_ge(r_set, 2 * t.n + h + 1)
                dve.wait_ge(h_summed, 2 * t.n + h + 1)
                if peeled is None or peeled >= 1:
                    dve.wait_ge(cand_set, 2 * t.n + h - 1)
                dve.scalar_tensor_tensor(out=pre[:, h], in0=h_ps,
                                         scalar=gate_bias[:, 1, 2 * KD + h:2 * KD + h + 1], in1=r[:, h],
                                         op0=ALU.add, op1=ALU.mult).then_inc(rh_set, 1)

            def add_i(t, h):
                dve.wait_ge(i_summed, 2 * t.n + h + 1)
                dve.wait_ge(rh_set, 2 * t.n + h + 1)
                dve.tensor_tensor(pre[:, h], i_ps, pre[:, h], ALU.add).then_inc(pre_set, 1)

            def update(t, h, peeled):
                dve.wait_ge(diff_set, 2 * t.n + h + 1)
                dve.wait_ge(z_set, 2 * t.n + h + 1)
                if peeled is None or peeled >= 1:
                    dve.wait_ge(new_turned, 2 * t.n + h - 1)
                dve.tensor_tensor(new[:, h], diff[:, h], z[:, h], ALU.mult).then_inc(zdiff_set, 1)
                dve.wait_ge(zdiff_set, 2 * t.n + h + 1)
                dve.tensor_tensor(new[:, h], new[:, h], cand[:, h], ALU.add).then_inc(new_set, 1)

            def statistics(t, which, rows, stats_set, norm_set, var_set):
                for j in range(ROWS):
                    dve.bn_stats(stats[:, which, j], rows[j]).then_inc(stats_set, 1)
                dve.wait_ge(stats_set, ROWS * (t.n + 1))
                gate.take_waits()
                for j in range(ROWS):
                    dve.bn_aggr(norm[:, which, j], stats[:, which, j]).then_inc(norm_set, 1)
                dve.wait_ge(norm_set, ROWS * (t.n + 1))
                dve.tensor_scalar(var_eps[:, which], norm[:, which, :, 1], EPS_NORM, None, ALU.add).then_inc(var_set, 1)

            def turn_shift(t, which, rstd_set, shift_set):
                dve.wait_ge(rstd_set, t.n + 1)
                dve.scalar_tensor_tensor(out=shift[:, which], in0=norm[:, which, :, 0], scalar=-1.0,
                                         in1=rstd[:, which], op0=ALU.mult, op1=ALU.mult).then_inc(shift_set, 1)

            def residual(t, peeled):
                dve.wait_ge(unit_set, t.n + 1)
                dve.tensor_tensor(scaled[:], unit[:], gamma_b[:].unsqueeze(1).to_broadcast([P, ROWS, D]),
                                  ALU.mult).then_inc(scaled_set, 1)
                dve.wait_ge(x_beta_set, t.n + 1)
                dve.wait_ge(scaled_set, t.n + 1)
                dve.tensor_tensor(resid[:, t.slot], scaled[:], x_beta[:, t.slot], ALU.add).then_inc(resid_set, 1)

            def step(t, peeled):
                u = t.at(-1)
                if peeled == 0:
                    invert_count(t)
                    invert_count(t.at(1))
                    low_mean(t)
                if gates(peeled):
                    reset_h(t, 0, peeled)
                    add_i(t, 0)
                if norms(peeled):
                    dve.wait_ge(new_turned, 2 * (u.n + 1))
                    statistics(u, 0, [back[:, j] for j in range(ROWS)], stats1_set, norm1_set, var1_set)
                    turn_shift(u, 0, rstd1_set, shift1_set)
                if gates(peeled):
                    update(t, 0, peeled)
                    reset_h(t, 1, peeled)
                if norms(peeled):
                    residual(u, peeled)
                if turns_next(peeled):
                    low_mean(t.at(1))
                if gates(peeled):
                    add_i(t, 1)
                if norms(peeled):
                    dve.wait_ge(resid_set, u.n + 1)
                    statistics(u, 1, [resid[:, u.slot, j] for j in range(ROWS)], stats2_set, norm2_set, var2_set)
                if gates(peeled):
                    update(t, 1, peeled)
                if norms(peeled):
                    if peeled is None or peeled >= 2:
                        dve.wait_ge(result_set, u.n)
                    turn_shift(u, 1, rstd2_set, shift2_set)
                if peeled is None or peeled + 2 < blocks:
                    invert_count(t.at(2))

            steps(dve, step)


_INS = ["x", "src", "dst", "L0_gnn_W1", "L0_gnn_b1", "L0_gnn_W2", "L0_gnn_b2", "L0_gnn_w_ih", "L0_gnn_w_hh",
        "L0_gnn_b_ih", "L0_gnn_b_hh", "L0_gnn_gamma", "L0_gnn_beta"]


def kernel(**inputs):
    import numpy as _np
    import concourse.bacc as _bacc
    from concourse import mybir as _mybir
    from concourse.bass_utils import run_bass_kernel_spmd as _run

    nc = _bacc.Bacc("TRN2", target_bir_lowering=False, num_devices=1)
    arrays, args = {}, []
    for name in _INS:
        a = _np.ascontiguousarray(inputs[name])
        arrays[f"in_{name}_dram"] = a
        args.append(nc.dram_tensor(f"in_{name}_dram", a.shape, _mybir.dt.from_np(a.dtype), kind="ExternalInput").ap())
    shape = inputs["x"].shape
    args.append(nc.dram_tensor("out_0_dram", shape, _mybir.dt.float32, kind="ExternalOutput").ap())
    gnn_layer(nc, *args)
    r = _run(nc, [arrays], core_ids=[0])
    return r.results[0]["out_0_dram"]
```
